# Optimizing a Trainium2 kernel written in Bass

```python
import numpy as np
import jax
import jax.numpy as jnp

def _softmax(x, axis=-1):
    return jax.nn.softmax(x, axis=axis)

def _gelu(x):
    return jax.nn.gelu(x, approximate=True)

def _silu(x):
    return jax.nn.silu(x)

def _sigmoid(x):
    return jax.nn.sigmoid(x)

def _layernorm(x, axis=-1, eps=1e-05):
    m = jnp.mean(x, axis=axis, keepdims=True)
    v = jnp.var(x, axis=axis, keepdims=True)
    return (x - m) / jnp.sqrt(v + eps)

def _scatter_add(tgt, idx, src, axis=0):
    return tgt.at[idx].add(src)

def _segment_sum(src, seg, n):
    return jax.ops.segment_sum(src, seg, n)
kernel_name = 'mk_cond_resid_d4_seqx_r8_0f8b9c'

def setup_inputs(seed: int=0):
    np.random.seed(seed)
    _w = jnp.asarray

    def _rec_inputs():
        import jax
        import jax.numpy as jnp
        _rk = jax.random.key(seed)
        x = -0.000125 + 0.9999 * jax.random.normal(jax.random.fold_in(_rk, 1), (8, 128, 512), jnp.float32)
        _lenS = 128 - jax.random.randint(jax.random.fold_in(_rk, 7), (8,), 0, max(1, 128 // 4) + 1, jnp.int32)
        _lenS2 = 128 - jax.random.randint(jax.random.fold_in(_rk, 8), (8,), 0, max(1, 128 // 4) + 1, jnp.int32)
        itok_B_0_23 = jax.random.randint(jax.random.fold_in(_rk, 11), (8,), 0, 24, jnp.int32)
        itok_B_0_15 = jax.random.randint(jax.random.fold_in(_rk, 12), (8,), 0, 16, jnp.int32)
        itok_B_3_7 = jax.random.randint(jax.random.fold_in(_rk, 13), (8,), 3, 8, jnp.int32)
        itok_Bx16_0_63 = jax.random.randint(jax.random.fold_in(_rk, 14), (8, 16), 0, 64, jnp.int32)
        itok_B_207_1644 = jax.random.randint(jax.random.fold_in(_rk, 15), (8,), 207, 1645, jnp.int32)
        return (x, itok_B_0_23, itok_B_0_15, itok_B_3_7, itok_Bx16_0_63, itok_B_207_1644)
    x, itok_B_0_23, itok_B_0_15, itok_B_3_7, itok_Bx16_0_63, itok_B_207_1644 = _rec_inputs()

    def _L0_cond_setup():
        import jax, jax.numpy as jnp
        import numpy as np
        R = 16
        ALPHA = 32
        SCALING = ALPHA / R
        SLOTS = 32
        IN_F = 512
        OUT_F = 512
        B, T = (8, 128)
        key = jax.random.key(seed)
        k1, k2, k3, k4, k5, k6 = jax.random.split(key, 6)
        x = jax.random.normal(k1, (B, T, IN_F), dtype=jnp.float32)
        adapter_mapping = jax.random.randint(k2, (B,), 0, SLOTS, dtype=jnp.int32)
        W = jax.random.normal(k3, (OUT_F, IN_F), dtype=jnp.float32) * 0.02
        b = jax.random.normal(k4, (OUT_F,), dtype=jnp.float32) * 0.02
        lora_As = jax.random.normal(k5, (SLOTS, IN_F, R), dtype=jnp.float32) * 0.02
        lora_Bs = jax.random.normal(k6, (SLOTS, R, OUT_F), dtype=jnp.float32) * 0.02
        return {'x': x, 'adapter_mapping': adapter_mapping, 'W': W, 'b': b, 'lora_As': lora_As, 'lora_Bs': lora_Bs}
    _L0_cond_all = _L0_cond_setup()
    _L0_cond_in = {k: v for k, v in _L0_cond_all.items() if k in ('W', 'b', 'lora_As', 'lora_Bs')}
    del _L0_cond_all

    def _L1_cond_setup():
        import jax, jax.numpy as jnp
        import numpy as np
        MAX_LORAS = 16
        IN, OUT = (512, 512)
        B, S = (8, 256)
        key = jax.random.key(seed)
        k1, k2, k3 = jax.random.split(key, 3)
        x = jax.random.normal(k1, (B, S, IN), dtype=jnp.float32)
        adapter_ids = jax.random.randint(k2, (B,), 0, MAX_LORAS)
        weight = jax.random.normal(k3, (MAX_LORAS, OUT, IN), dtype=jnp.float32) * 0.02
        return {'x': x, 'adapter_ids': adapter_ids, 'weight': weight}
    _L1_cond_all = _L1_cond_setup()
    _L1_cond_in = {k: v for k, v in _L1_cond_all.items() if k in ('weight',)}
    del _L1_cond_all

    def _L2_cond_setup():
        import jax, jax.numpy as jnp
        import numpy as np
        RANK = 16
        ALPHA = 16.0
        SCALING = ALPHA / RANK
        N_ADAPTERS = 8
        IN_F = 512
        OUT_F = 512
        BATCH = 4
        SEQ = 256
        key = jax.random.key(seed)
        kx, ka, kb, ki = jax.random.split(key, 4)
        x = jax.random.normal(kx, (BATCH, SEQ, IN_F), dtype=jnp.float32)
        A = jax.random.normal(ka, (N_ADAPTERS, OUT_F, RANK), dtype=jnp.float32) * 0.02
        B = jax.random.normal(kb, (N_ADAPTERS, RANK, IN_F), dtype=jnp.float32) * 0.02
        adapter_ids = jax.random.randint(ki, (BATCH,), 0, N_ADAPTERS, dtype=jnp.int32)
        return {'x': x, 'A': A, 'B': B, 'adapter_ids': adapter_ids}
    _L2_cond_all = _L2_cond_setup()
    _L2_cond_in = {k: v for k, v in _L2_cond_all.items() if k in ('A', 'B')}
    del _L2_cond_all

    def _L3_cond_setup():
        import jax, jax.numpy as jnp
        import numpy as np
        B, S, HID = (4, 128, 512)
        D, HQ, HK = (128, 32, 8)
        PAGES, PSIZE, NPP = (64, 32, 16)
        THETA = 10000.0
        EPS = 1e-06
        SCALE = 1.0 / float(np.sqrt(D))

        def _rmsnorm(t, w):
            var = jnp.mean(t * t, axis=-1, keepdims=True)
            return t * jax.lax.rsqrt(var + EPS) * w

        def _rope(t, pos):
            inv_freq = 1.0 / THETA ** (jnp.arange(0, D, 2, dtype=jnp.float32) / D)
            freqs = pos[..., None].astype(jnp.float32) * inv_freq
            cos = jnp.cos(freqs)[:, :, None, :]
            sin = jnp.sin(freqs)[:, :, None, :]
            t1, t2 = (t[..., :D // 2], t[..., D // 2:])
            return jnp.concatenate([t1 * cos - t2 * sin, t2 * cos + t1 * sin], axis=-1)
        key = jax.random.key(seed)
        ks = jax.random.split(key, 10)
        x = jax.random.normal(ks[0], (B, S, HID), jnp.float32)
        Wq = jax.random.normal(ks[1], (HQ * D, HID), jnp.float32) * 0.02
        Wk = jax.random.normal(ks[2], (HK * D, HID), jnp.float32) * 0.02
        Wv = jax.random.normal(ks[3], (HK * D, HID), jnp.float32) * 0.02
        Wo = jax.random.normal(ks[4], (HID, HQ * D), jnp.float32) * 0.02
        q_norm_w = jax.random.uniform(ks[5], (D,), jnp.float32)
        k_norm_w = jax.random.uniform(ks[6], (D,), jnp.float32)
        k_cache = jax.random.normal(ks[7], (PAGES, PSIZE, HK, D), jnp.float32)
        v_cache = jax.random.normal(ks[8], (PAGES, PSIZE, HK, D), jnp.float32)
        block_table = jnp.arange(B * NPP, dtype=jnp.int32).reshape(B, NPP)
        cache_seqlens = jax.random.randint(ks[9], (B,), 0, 475).astype(jnp.int32)
        return dict(x=x, Wq=Wq, Wk=Wk, Wv=Wv, Wo=Wo, q_norm_w=q_norm_w, k_norm_w=k_norm_w, k_cache=k_cache, v_cache=v_cache, block_table=block_table, cache_seqlens=cache_seqlens)
    _L3_cond_all = _L3_cond_setup()
    _L3_cond_in = {k: v for k, v in _L3_cond_all.items() if k in ('Wq', 'Wk', 'Wv', 'Wo', 'q_norm_w', 'k_norm_w', 'k_cache', 'v_cache')}
    del _L3_cond_all
    return {'x': x, 'itok_B_0_23': itok_B_0_23, 'itok_B_0_15': itok_B_0_15, 'itok_B_3_7': itok_B_3_7, 'itok_Bx16_0_63': itok_Bx16_0_63, 'itok_B_207_1644': itok_B_207_1644, 'L0_cond_W': _L0_cond_in['W'], 'L0_cond_b': _L0_cond_in['b'], 'L0_cond_lora_As': _L0_cond_in['lora_As'], 'L0_cond_lora_Bs': _L0_cond_in['lora_Bs'], 'L1_cond_weight': _L1_cond_in['weight'], 'L2_cond_A': _L2_cond_in['A'], 'L2_cond_B': _L2_cond_in['B'], 'L3_cond_Wq': _L3_cond_in['Wq'], 'L3_cond_Wk': _L3_cond_in['Wk'], 'L3_cond_Wv': _L3_cond_in['Wv'], 'L3_cond_Wo': _L3_cond_in['Wo'], 'L3_cond_q_norm_w': _L3_cond_in['q_norm_w'], 'L3_cond_k_norm_w': _L3_cond_in['k_norm_w'], 'L3_cond_k_cache': _L3_cond_in['k_cache'], 'L3_cond_v_cache': _L3_cond_in['v_cache']}

def reference(x, itok_B_0_23, itok_B_0_15, itok_B_3_7, itok_Bx16_0_63, itok_B_207_1644, L0_cond_W, L0_cond_b, L0_cond_lora_As, L0_cond_lora_Bs, L1_cond_weight, L2_cond_A, L2_cond_B, L3_cond_Wq, L3_cond_Wk, L3_cond_Wv, L3_cond_Wo, L3_cond_q_norm_w, L3_cond_k_norm_w, L3_cond_k_cache, L3_cond_v_cache):
    import jax
    import jax.numpy as jnp

    def _L0_cond_ref(x, adapter_mapping, W, b, lora_As, lora_Bs):
        import jax, jax.numpy as jnp
        import numpy as np
        R = 16
        ALPHA = 32
        SCALING = ALPHA / R
        SLOTS = 32
        IN_F = 512
        OUT_F = 512
        B, T = (8, 128)
        base_out = jnp.einsum('bti,oi->bto', x, W) + b
        A = lora_As[adapter_mapping]
        Bm = lora_Bs[adapter_mapping]
        lora_h = jnp.einsum('bti,bir->btr', x, A)
        lora_out = jnp.einsum('btr,bro->bto', lora_h, Bm)
        return base_out + lora_out * SCALING

    def _L1_cond_ref(x, adapter_ids, weight):
        import jax, jax.numpy as jnp
        import numpy as np
        MAX_LORAS = 16
        IN, OUT = (512, 512)
        B, S = (8, 256)
        w = weight[adapter_ids]
        return jnp.einsum('bsi,boi->bso', x, w)

    def _L2_cond_ref(x, A, B, adapter_ids):
        import jax, jax.numpy as jnp
        import numpy as np
        RANK = 16
        ALPHA = 16.0
        SCALING = ALPHA / RANK
        N_ADAPTERS = 8
        IN_F = 512
        OUT_F = 512
        BATCH = 4
        SEQ = 256
        B_sel = B[adapter_ids]
        A_sel = A[adapter_ids]
        Bx = jnp.einsum('bni,bri->bnr', x, B_sel)
        out = jnp.einsum('bnr,bor->bno', Bx, A_sel)
        return out * SCALING

    def _L3_cond_ref(x, Wq, Wk, Wv, Wo, q_norm_w, k_norm_w, k_cache, v_cache, block_table, cache_seqlens):
        import jax, jax.numpy as jnp
        import numpy as np
        B, S, HID = (4, 128, 512)
        D, HQ, HK = (128, 32, 8)
        PAGES, PSIZE, NPP = (64, 32, 16)
        THETA = 10000.0
        EPS = 1e-06
        SCALE = 1.0 / float(np.sqrt(D))

        def _rmsnorm(t, w):
            var = jnp.mean(t * t, axis=-1, keepdims=True)
            return t * jax.lax.rsqrt(var + EPS) * w

        def _rope(t, pos):
            inv_freq = 1.0 / THETA ** (jnp.arange(0, D, 2, dtype=jnp.float32) / D)
            freqs = pos[..., None].astype(jnp.float32) * inv_freq
            cos = jnp.cos(freqs)[:, :, None, :]
            sin = jnp.sin(freqs)[:, :, None, :]
            t1, t2 = (t[..., :D // 2], t[..., D // 2:])
            return jnp.concatenate([t1 * cos - t2 * sin, t2 * cos + t1 * sin], axis=-1)
        bsz, seqlen, _ = x.shape
        q = jnp.einsum('bsd,ed->bse', x, Wq).reshape(bsz, seqlen, HQ, D)
        k = jnp.einsum('bsd,ed->bse', x, Wk).reshape(bsz, seqlen, HK, D)
        v = jnp.einsum('bsd,ed->bse', x, Wv).reshape(bsz, seqlen, HK, D)
        q = _rmsnorm(q, q_norm_w)
        k = _rmsnorm(k, k_norm_w)
        pos = cache_seqlens[:, None] + jnp.arange(seqlen)[None, :]
        q = _rope(q, pos)
        k = _rope(k, pos)
        L = NPP * PSIZE
        kc = k_cache[block_table].reshape(bsz, L, HK, D)
        vc = v_cache[block_table].reshape(bsz, L, HK, D)
        k_all = jnp.concatenate([kc, k], axis=1)
        v_all = jnp.concatenate([vc, v], axis=1)
        valid_c = jnp.arange(L)[None, :] < cache_seqlens[:, None]
        valid = jnp.concatenate([valid_c, jnp.ones((bsz, seqlen), dtype=bool)], axis=1)
        rep = HQ // HK
        k_all = jnp.repeat(k_all, rep, axis=2)
        v_all = jnp.repeat(v_all, rep, axis=2)
        scores = jnp.einsum('bqhd,bkhd->bhqk', q, k_all) * SCALE
        scores = jnp.where(valid[:, None, None, :], scores, -1e+30)
        probs = jax.nn.softmax(scores, axis=-1)
        o = jnp.einsum('bhqk,bkhd->bqhd', probs, v_all)
        o = o.reshape(bsz, seqlen, HQ * D)
        return jnp.einsum('bse,de->bsd', o, Wo)
    x = x + _L0_cond_ref(x, itok_B_0_23, L0_cond_W, L0_cond_b, L0_cond_lora_As, L0_cond_lora_Bs)
    x = x + _L1_cond_ref(x, itok_B_0_15, L1_cond_weight)
    x = x + _L2_cond_ref(x, L2_cond_A, L2_cond_B, itok_B_3_7)
    x = x + _L3_cond_ref(x, L3_cond_Wq, L3_cond_Wk, L3_cond_Wv, L3_cond_Wo, L3_cond_q_norm_w, L3_cond_k_norm_w, L3_cond_k_cache, L3_cond_v_cache, itok_Bx16_0_63, itok_B_207_1644)
    return x

_drawn_inputs = setup_inputs


def setup_inputs(seed=0):
    import zlib

    import numpy as np

    out = dict(_drawn_inputs(seed))
    spreads = {}
    factors = {'L0_cond_b': 3.297,
     'L3_cond_Wk': 24.888,
     'L3_cond_Wv': 34.433,
     'L3_cond_q_norm_w': 3.367,
     'L3_cond_k_norm_w': 22.362,
     'L3_cond_k_cache': 8.0,
     'L3_cond_v_cache': 8.0}
    for name, (base, spread) in spreads.items():
        noise = np.random.default_rng([zlib.crc32(name.encode()), seed]).standard_normal(out[name].shape)
        drawn = base * np.exp(spread * noise) if base else spread * noise
        out[name] = jnp.asarray(drawn.astype(out[name].dtype))
    for name, factor in factors.items():
        out[name] = (out[name] * factor).astype(out[name].dtype)
    return out
```

```python
from contextlib import ExitStack

import numpy as np

import concourse.bass as bass
from concourse import mybir

ALU = mybir.AluOpType
ACT = mybir.ActivationFunctionType
F32 = mybir.dt.float32
F32R = mybir.dt.float32r
I32 = mybir.dt.int32

P = 128
B = 8
HID = 512
KT = HID // P
RANK = 16
SLOTS0, SLOTS1, SLOTS2 = 32, 16, 8
HQ, HK, D = 32, 8, 128
GROUP = HQ // HK
PAGES, PSIZE, NPP = 64, 32, 16
CACHE = NPP * PSIZE
CCH = CACHE // P
CH = CCH + 1
KEYS = CACHE + P
ROWS_PER_PAGE = PSIZE // CCH
UNITS = HK * B
WQKV = GROUP * D + 2 * D
WCOLS = KT * WQKV + GROUP * HID
WCH = WCOLS // B
AHEAD = B + 1
THETA = 10000.0
EPS = 1e-06
SCALE = 1.0 / float(np.sqrt(D))
LORA_SCALE = 2.0
NEG = -1e30
TWO_PI = 2.0 * np.pi
TURN_A = 6.28125
TURN_B = float(np.float32(np.round((TWO_PI - TURN_A) * 2.0**21) / 2.0**21))
TURN_C = float(TWO_PI - TURN_A - TURN_B)
ROUND_MAGIC = 1.5 * 2.0**23
PI_BELOW = float(np.nextafter(np.float32(np.pi), np.float32(0.0)))


def build(nc, x, x_t, ids0, ids1, ids2, table, lens, w0_t, bias0, lora_a, lora_b, w1_t, w2_b, w2_a,
          w_qkvo, q_norm, k_norm, k_rows, v_rows, inv_freq, row_in_table, ident_in, out):
    ctx = ExitStack()
    with ctx:
        def sem(name):
            return ctx.enter_context(nc.semaphore(name))

        def sb(name, shape, dt=F32, scope=ctx):
            return scope.enter_context(nc.sbuf_tensor(name, shape, dt))

        def pb(name, shape, scope=ctx):
            return scope.enter_context(nc.psum_tensor(name, shape, F32))

        w_hi = sb("w_hi", [P, 2, WCOLS], F32R)
        w_lo = sb("w_lo", [P, 2, WCOLS], F32R)
        w_raw = sb("w_raw", [P, WCH])
        y = sb("y", [P, B, HID])
        cos_q = sb("cos_q", [P, B, D])
        sin_q = sb("sin_q", [P, B, D])
        cos_k = sb("cos_k", [P, B, D])
        sin_k = sb("sin_k", [P, B, D])
        ident = sb("ident", [P, P])
        pos = sb("pos", [P, CACHE])
        len_f = sb("len_f", [P, B])
        row_id = sb("row_id", [P, UNITS], I32)
        neg_half = sb("neg_half", [P, GROUP + 1])
        xt_dram = nc.dram_tensor("xt_split", [B, P, 2, HID], F32).ap()

        w_first_in = sem("w_first_in")
        w_raw_in = sem("w_raw_in")
        w_split = sem("w_split")
        w_rounded = sem("w_rounded")
        tables_in = sem("tables_in")

        def w_home(chunk):
            return ((chunk >> 3) & 1) * WCOLS + (chunk & 7) * WCH

        w_hi_flat = w_hi[:, :, :].rearrange("p s c -> p (s c)")
        w_lo_flat = w_lo[:, :, :].rearrange("p s c -> p (s c)")

        def split_weights(pool, chunk, arrived, count):
            pool.wait_ge(arrived, 16 * count)
            hi = w_hi_flat[:, bass.ds(w_home(chunk), WCH)]
            lo = w_lo_flat[:, bass.ds(w_home(chunk), WCH)]
            pool.nop(nofuse=True)
            nc.gpsimd.tensor_copy(hi, w_raw[:, :]).then_inc(w_rounded, 1)
            pool.wait_ge(w_rounded, chunk + 1)
            nc.gpsimd.tensor_tensor(lo, w_raw[:, :], hi.bitcast(F32), ALU.subtract).then_inc(w_split, 1)

        with ExitStack() as p1:
            w0 = sb("w0", [P, KT, HID], scope=p1)
            w1 = sb("w1", [P, KT, HID], scope=p1)
            xb = sb("xb", [P, HID], scope=p1)
            xbt = sb("xbt", [P, HID], scope=p1)
            a0 = sb("a0", [P, KT, RANK], scope=p1)
            b0 = sb("b0", [RANK + 1, HID], scope=p1)
            b2 = sb("b2", [P, KT, RANK], scope=p1)
            a2 = sb("a2", [RANK, HID], scope=p1)
            h0 = sb("h0", [RANK + 1, P], scope=p1)
            h2 = sb("h2", [RANK, P], scope=p1)
            x1 = sb("x1", [P, HID], scope=p1)
            x2 = sb("x2", [P, HID], scope=p1)
            x3 = sb("x3", [P, HID], scope=p1)
            x1t = sb("x1t", [P, HID], scope=p1)
            x2t = sb("x2t", [P, HID], scope=p1)
            x3t = sb("x3t", [P, 2, HID], F32R, scope=p1)
            ids = sb("ids", [1, 3, B], I32, scope=p1)
            len_i = sb("len_i", [P, B], I32, scope=p1)
            tab_i = sb("tab_i", [P, B], I32, scope=p1)
            part_row = sb("part_row", [P, UNITS], I32, scope=p1)
            tab8 = sb("tab8", [P, B], I32, scope=p1)
            freq = sb("freq", [P, D // 2], scope=p1)
            wq_row = sb("wq_row", [P, D], scope=p1)
            wk_row = sb("wk_row", [P, D], scope=p1)
            row_f = sb("row_f", [P, B], scope=p1)
            ang = sb("ang", [P, B, D // 2], scope=p1)
            turns = sb("turns", [P, B, D // 2], scope=p1)
            red = sb("red", [P, B, D // 2], scope=p1)
            sin_t = sb("sin_t", [P, B, D // 2], scope=p1)
            cos_t = sb("cos_t", [P, B, D // 2], scope=p1)

            ps_l0 = pb("ps_l0", [P, HID], p1)
            ps_l1 = pb("ps_l1", [P, HID], p1)
            ps_l2 = pb("ps_l2", [P, HID], p1)
            ps_h0 = pb("ps_h0", [P, HID], p1)
            ps_h2 = pb("ps_h2", [P, HID], p1)
            ps_t = pb("ps_t", [P, HID], p1)

            def psem(name):
                return p1.enter_context(nc.semaphore(name))

            w0_in, ids_in = psem("w0_in"), psem("ids_in")
            x_in, xt_in, ab0_in, w1_in, ab2_in = (psem(s) for s in ("x_in", "xt_in", "ab0_in", "w1_in", "ab2_in"))
            ones_set, pos_set = psem("ones_set"), psem("pos_set")
            h0_done, h0_out, l0_done, x1_out = (psem(s) for s in ("h0_done", "h0_out", "l0_done", "x1_out"))
            t1_done, t1_out, l1_done, x2_out = (psem(s) for s in ("t1_done", "t1_out", "l1_done", "x2_out"))
            t2_done, t2_out, h2_done, h2_out = (psem(s) for s in ("t2_done", "t2_out", "h2_done", "h2_out"))
            l2_done, x3_out, y_out, t3_done = (psem(s) for s in ("l2_done", "x3_out", "y_out", "t3_done"))
            t3_hi, t3_lo, xt_stored = (psem(s) for s in ("t3_hi", "t3_lo", "xt_stored"))
            dve_step, trig_arg, trig_done = (psem(s) for s in ("dve_step", "trig_arg", "trig_done"))
            neg_half_set = psem("neg_half_set")

            with nc.Block() as block:
                @block.sync
                def _(sp):
                    sp.dma_start(ids[:, 0, :], ids0).then_inc(ids_in, 16)
                    sp.dma_start(ids[:, 1, :], ids1).then_inc(ids_in, 16)
                    sp.dma_start(ids[:, 2, :], ids2).then_inc(ids_in, 16)
                    sp.dma_start(w0[:, :, :], w0_t).then_inc(w0_in, 16)
                    sp.dma_start(b0[RANK:RANK + 1, :], bias0).then_inc(w0_in, 16)
                    sp.wait_ge(ids_in, 48)
                    with sp.Fori(0, B) as b:
                        sp.wait_ge(l0_done, b)
                        sp.dma_start(xbt[:, :], x_t[bass.ds(b, 1), :, :].rearrange("a p c -> p (a c)")).then_inc(xt_in, 16)
                        sp.nop(nofuse=True)
                        id0 = sp.value_load(ids[0:1, 0, bass.ds(b, 1)], min_val=0, max_val=SLOTS0 - 1)
                        sp.dma_start(a0[:, :, :], lora_a[bass.ds(id0, 1), :, :, :].rearrange("a p k r -> p (a k) r")).then_inc(ab0_in, 16)
                        sp.dma_start(b0[0:RANK, :], lora_b[bass.ds(id0, 1), :, :].rearrange("a r c -> (a r) c")).then_inc(ab0_in, 16)
                        sp.wait_ge(x1_out, b)
                        sp.dma_start(xb[:, :], x[bass.ds(b, 1), :, :].rearrange("a p c -> p (a c)")).then_inc(x_in, 16)
                        sp.wait_ge(l1_done, b)
                        sp.nop(nofuse=True)
                        id1 = sp.value_load(ids[0:1, 1, bass.ds(b, 1)], min_val=0, max_val=SLOTS1 - 1)
                        sp.dma_start(w1[:, :, :], w1_t[bass.ds(id1, 1), :, :, :].rearrange("a p k c -> p (a k) c")).then_inc(w1_in, 16)
                        sp.wait_ge(l2_done, b)
                        sp.nop(nofuse=True)
                        id2 = sp.value_load(ids[0:1, 2, bass.ds(b, 1)], min_val=0, max_val=SLOTS2 - 1)
                        sp.dma_start(b2[:, :, :], w2_b[bass.ds(id2, 1), :, :, :].rearrange("a p k r -> p (a k) r")).then_inc(ab2_in, 16)
                        sp.dma_start(a2[:, :], w2_a[bass.ds(id2, 1), :, :].rearrange("a r c -> (a r) c")).then_inc(ab2_in, 16)

                @block.gpsimd
                def _(pool):
                    nc.gpsimd.iota(pos[:, :], [[1, CCH], [CCH, P]], base=0, channel_multiplier=0,
                                   allow_small_or_imprecise_dtypes=True).then_inc(pos_set, 1)
                    nc.gpsimd.iota(row_f[:, :], [[0, B]], base=0, channel_multiplier=1,
                                   allow_small_or_imprecise_dtypes=True).then_inc(pos_set, 1)
                    nc.gpsimd.memset(neg_half[:, :], -0.5).then_inc(neg_half_set, 1)
                    with pool.Fori(0, AHEAD) as c:
                        pool.dma_start(w_raw[:, :], w_qkvo[bass.ds(c, 1), :, :].rearrange("a p c -> p (a c)")).then_inc(w_first_in, 16)
                        split_weights(pool, c, w_first_in, c + 1)
                        pool.wait_ge(w_split, c + 1)

                @block.scalar
                def _(act):
                    act.dma_start(ident[:, :], ident_in).then_inc(tables_in, 16)
                    act.dma_start(len_i[:, :], lens.partition_broadcast(P)).then_inc(tables_in, 16)
                    act.dma_start(tab_i[:, :], table).then_inc(tables_in, 16)
                    act.dma_start(part_row[:, :], row_in_table).then_inc(tables_in, 16)
                    act.dma_start(freq[:, :], inv_freq.partition_broadcast(P)).then_inc(tables_in, 16)
                    act.dma_start(wq_row[:, :], q_norm.partition_broadcast(P)).then_inc(tables_in, 16)
                    act.dma_start(wk_row[:, :], k_norm.partition_broadcast(P)).then_inc(tables_in, 16)
                    act.wait_ge(trig_arg, 1)
                    nc.scalar.activation(sin_t[:, :, :], red[:, :, :], ACT.Sin).then_inc(trig_done, 1)
                    act.wait_ge(trig_arg, 2)
                    nc.scalar.activation(cos_t[:, :, :], red[:, :, :], ACT.Sin).then_inc(trig_done, 1)
                    with act.Fori(0, B) as b:
                        act.wait_ge(h0_done, b + 1)
                        act.wait_ge(l0_done, b)
                        nc.scalar.activation(h0[0:RANK, :], ps_h0[0:RANK, 0:P], ACT.Copy, scale=LORA_SCALE).then_inc(h0_out, 1)
                        act.wait_ge(t1_done, b + 1)
                        act.wait_ge(l1_done, b)
                        nc.scalar.activation(x1t[:, :], ps_t[:, :], ACT.Copy).then_inc(t1_out, 1)
                        act.wait_ge(t2_done, b + 1)
                        act.wait_ge(h2_done, b)
                        nc.scalar.activation(x2t[:, :], ps_t[:, :], ACT.Copy).then_inc(t2_out, 1)
                        act.wait_ge(h2_done, b + 1)
                        act.wait_ge(l2_done, b)
                        nc.scalar.activation(h2[:, :], ps_h2[0:RANK, 0:P], ACT.Copy).then_inc(h2_out, 1)
                        act.wait_ge(t3_done, b + 1)
                        act.wait_ge(xt_stored, 16 * b)
                        nc.scalar.activation(x3t[:, 0, :], ps_t[:, :], ACT.Copy).then_inc(t3_hi, 1)
                        act.wait_ge(t3_lo, b + 1)
                        act.dma_start(xt_dram[bass.ds(b, 1), :, :, :].rearrange("a p s c -> p (a s) c"), x3t[:, :, :].bitcast(F32)).then_inc(xt_stored, 16)
                    act.wait_ge(xt_stored, 16 * B)

                @block.tensor
                def _(pe):
                    pe.wait_ge(w0_in, 32)
                    pe.wait_ge(tables_in, 16 * 7)
                    pe.wait_ge(ones_set, 1)

                    def turn(src, done):
                        for k in range(KT):
                            mm = nc.tensor.transpose(ps_t[:, k * P:(k + 1) * P], src[:, k * P:(k + 1) * P], ident[:, :])
                        mm.then_inc(done, 1)

                    with pe.Fori(0, B) as b:
                        pe.wait_ge(xt_in, 16 * (b + 1))
                        pe.wait_ge(ab0_in, 32 * (b + 1))
                        for k in range(KT):
                            mm = nc.tensor.matmul(ps_h0[0:RANK, 0:P], a0[:, k, :], xbt[:, k * P:(k + 1) * P],
                                                  start=(k == 0), stop=(k == KT - 1))
                        mm.then_inc(h0_done, 1)
                        pe.wait_ge(x1_out, b)
                        for k in range(KT):
                            nc.tensor.matmul(ps_l0[:, :], xbt[:, k * P:(k + 1) * P], w0[:, k, :],
                                             start=(k == 0), stop=False)
                        pe.wait_ge(h0_out, b + 1)
                        nc.tensor.matmul(ps_l0[:, :], h0[:, :], b0[:, :], start=False, stop=True).then_inc(l0_done, 1)
                        pe.wait_ge(x1_out, b + 1)
                        pe.wait_ge(t3_lo, b)
                        turn(x1, t1_done)
                        pe.wait_ge(t1_out, b + 1)
                        pe.wait_ge(w1_in, 16 * (b + 1))
                        for k in range(KT):
                            mm = nc.tensor.matmul(ps_l1[:, :], x1t[:, k * P:(k + 1) * P], w1[:, k, :],
                                                  start=(k == 0), stop=(k == KT - 1))
                        mm.then_inc(l1_done, 1)
                        pe.wait_ge(x2_out, b + 1)
                        turn(x2, t2_done)
                        pe.wait_ge(t2_out, b + 1)
                        pe.wait_ge(ab2_in, 32 * (b + 1))
                        for k in range(KT):
                            mm = nc.tensor.matmul(ps_h2[0:RANK, 0:P], b2[:, k, :], x2t[:, k * P:(k + 1) * P],
                                                  start=(k == 0), stop=(k == KT - 1))
                        mm.then_inc(h2_done, 1)
                        pe.wait_ge(h2_out, b + 1)
                        nc.tensor.matmul(ps_l2[:, :], h2[:, :], a2[:, :], start=True, stop=True).then_inc(l2_done, 1)
                        pe.wait_ge(x3_out, b + 1)
                        turn(x3, t3_done)

                @block.vector
                def _(dve):
                    steps = [0]

                    def step(ins):
                        steps[0] += 1
                        ins.then_inc(dve_step, 1)
                        dve.wait_ge(dve_step, steps[0])

                    nc.vector.memset(h0[:, :], 1.0).then_inc(ones_set, 1)
                    dve.wait_ge(tables_in, 16 * 7)
                    dve.wait_ge(pos_set, 2)
                    step(nc.vector.tensor_copy(len_f[:, :], len_i[:, :]))
                    step(nc.vector.tensor_scalar(tab8[:, :], tab_i[:, :], float(ROWS_PER_PAGE), None, ALU.mult))
                    step(nc.vector.tensor_tensor(
                        row_id[:, :].rearrange("p (g b) -> p g b", g=HK), part_row[:, :].rearrange("p (g b) -> p g b", g=HK),
                        tab8[:, :].rearrange("p (g b) -> p g b", g=1).broadcast_to([P, HK, B]), ALU.add))
                    step(nc.vector.tensor_tensor(row_f[:, :], row_f[:, :], len_f[:, :], ALU.add))
                    step(nc.vector.tensor_tensor(
                        ang[:, :, :], row_f[:, :].rearrange("p (b d) -> p b d", d=1).broadcast_to([P, B, D // 2]),
                        freq[:, :].rearrange("p (b d) -> p b d", b=1).broadcast_to([P, B, D // 2]), ALU.mult))

                    def reduce_angle(quarter):
                        step(nc.vector.tensor_scalar(turns[:, :, :], ang[:, :, :], 1.0 / TWO_PI, 0.25 * quarter, ALU.mult, ALU.add))
                        step(nc.vector.tensor_scalar(turns[:, :, :], turns[:, :, :], ROUND_MAGIC, None, ALU.add))
                        step(nc.vector.tensor_scalar(turns[:, :, :], turns[:, :, :], ROUND_MAGIC, None, ALU.subtract))
                        step(nc.vector.scalar_tensor_tensor(red[:, :, :], turns[:, :, :], -TURN_A, ang[:, :, :], ALU.mult, ALU.add))
                        step(nc.vector.scalar_tensor_tensor(red[:, :, :], turns[:, :, :], -TURN_B, red[:, :, :], ALU.mult, ALU.add))
                        step(nc.vector.scalar_tensor_tensor(red[:, :, :], turns[:, :, :], -TURN_C, red[:, :, :], ALU.mult, ALU.add))
                        step(nc.vector.tensor_scalar(red[:, :, :], red[:, :, :], 0.5 * np.pi * quarter, PI_BELOW, ALU.add, ALU.min))
                        nc.vector.tensor_scalar(red[:, :, :], red[:, :, :], -PI_BELOW, None, ALU.max).then_inc(trig_arg, 1)

                    reduce_angle(0)
                    dve.wait_ge(trig_done, 1)
                    reduce_angle(1)
                    dve.wait_ge(trig_done, 2)
                    half = D // 2
                    for w, cs, sn in ((wq_row, cos_q, sin_q), (wk_row, cos_k, sin_k)):
                        for o in (0, 1):
                            here = slice(o * half, (o + 1) * half)
                            there = slice((1 - o) * half, (2 - o) * half)

                            def wide(s):
                                return w[:, s].rearrange("p (b d) -> p b d", b=1).broadcast_to([P, B, half])

                            nc.vector.tensor_tensor(cs[:, :, here], cos_t[:, :, :], wide(here), ALU.mult)
                            nc.vector.scalar_tensor_tensor(sn[:, :, here], sin_t[:, :, :], -1.0 if o == 0 else 1.0,
                                                           wide(there), ALU.mult, ALU.mult)
                    with dve.Fori(0, B) as b:
                        dve.wait_ge(l0_done, b + 1)
                        dve.wait_ge(x_in, 16 * (b + 1))
                        dve.wait_ge(t1_done, b)
                        nc.vector.tensor_tensor(x1[:, :], ps_l0[:, :], xb[:, :], ALU.add).then_inc(x1_out, 1)
                        dve.wait_ge(l1_done, b + 1)
                        dve.wait_ge(x1_out, b + 1)
                        nc.vector.tensor_tensor(x2[:, :], ps_l1[:, :], x1[:, :], ALU.add).then_inc(x2_out, 1)
                        dve.wait_ge(l2_done, b + 1)
                        dve.wait_ge(x2_out, b + 1)
                        dve.wait_ge(y_out, b)
                        nc.vector.tensor_tensor(x3[:, :], ps_l2[:, :], x2[:, :], ALU.add).then_inc(x3_out, 1)
                        dve.wait_ge(x3_out, b + 1)
                        nc.vector.tensor_copy(y[:, bass.ds(b, 1), :].rearrange("p a c -> p (a c)"), x3[:, :]).then_inc(y_out, 1)
                        dve.wait_ge(t3_hi, b + 1)
                        nc.vector.tensor_tensor(x3t[:, 1, :], ps_t[:, :], x3t[:, 0, :].bitcast(F32), ALU.subtract).then_inc(t3_lo, 1)

        with ExitStack() as p2:
            x_s = sb("x_s", [P, 2, HID], F32R, scope=p2)
            k_raw = sb("k_raw", [P, CCH * D], scope=p2)
            v_raw = sb("v_raw", [P, CCH * D], scope=p2)
            row_s = sb("row_s", [P, 1], I32, scope=p2)
            kt_hi = sb("kt_hi", [P, KEYS], F32R, scope=p2)
            kt_lo = sb("kt_lo", [P, KEYS], F32R, scope=p2)
            v_hi = sb("v_hi", [P, CH, D], F32R, scope=p2)
            v_lo = sb("v_lo", [P, CH, D], F32R, scope=p2)
            qt_hi = sb("qt_hi", [P, GROUP * P], F32R, scope=p2)
            qt_lo = sb("qt_lo", [P, GROUP * P], F32R, scope=p2)
            prob = sb("prob", [P, GROUP, KEYS], scope=p2)
            pt_hi = sb("pt_hi", [P, CH, GROUP * P], F32R, scope=p2)
            pt_lo = sb("pt_lo", [P, CH, GROUP * P], F32R, scope=p2)
            ot_hi = sb("ot_hi", [P, GROUP * P], F32R, scope=p2)
            ot_lo = sb("ot_lo", [P, GROUP * P], F32R, scope=p2)
            rot_a = sb("rot_a", [P, GROUP + 1, D], scope=p2)
            rot_b = sb("rot_b", [P, GROUP + 1, D], scope=p2)
            rot = sb("rot", [P, GROUP + 1, D], scope=p2)
            mask = sb("mask", [P, P + CACHE + P], scope=p2)
            junk = sb("junk", [P, GROUP + 1, D], scope=p2)
            sq = sb("sq", [P, GROUP + 1], scope=p2)
            var = sb("var", [P, GROUP + 1], scope=p2)
            rstd = sb("rstd", [P, GROUP + 1], scope=p2)
            q_gain = sb("q_gain", [P, GROUP], scope=p2)
            low = sb("low", [P, GROUP], scope=p2)
            total = sb("total", [P, GROUP], scope=p2)
            inv = sb("inv", [P, GROUP], scope=p2)

            ps_s = pb("ps_s", [P, 3 * 512], p2)
            ps_ring = pb("ps_ring", [P, 2, 512], p2)
            ps_q = pb("ps_q", [P, 512], p2)
            ps_kv = pb("ps_kv", [P, 512], p2)
            ps_o = pb("ps_o", [P, 512], p2)

            def psem(name):
                return p2.enter_context(nc.semaphore(name))

            x_s_in, k_in, v_in = psem("x_s_in"), psem("k_in"), psem("v_in")
            row_set, mask_set, blank_set = psem("row_set"), psem("mask_set"), psem("blank_set")
            q_proj, kv_proj = psem("q_proj"), psem("kv_proj")
            sq_done, var_done, rstd_done, gain_done = (psem(s) for s in ("sq_done", "var_done", "rstd_done", "gain_done"))
            rot_done, rot_sum, rot_turned = psem("rot_done"), psem("rot_sum"), psem("rot_turned")
            qt_hi_out, qt_lo_out = psem("qt_hi_out"), psem("qt_lo_out")
            kc_turned, kc_hi_out, kc_lo_out = psem("kc_turned"), psem("kc_hi_out"), psem("kc_lo_out")
            v_round, v_split, vn_hi_out, vn_lo_out = (psem(s) for s in ("v_round", "v_split", "vn_hi_out", "vn_lo_out"))
            scores, low_done, exp_done, inv_done, prob_done = (psem(s) for s in ("scores", "low_done", "exp_done", "inv_done", "prob_done"))
            p_turned, pt_hi_out, pt_lo_out = psem("p_turned"), psem("pt_hi_out"), psem("pt_lo_out")
            pv_done, ot_hi_out, ot_lo_out = psem("pv_done"), psem("ot_hi_out"), psem("ot_lo_out")
            out_proj, y_added, out_in = psem("out_proj"), psem("y_added"), psem("out_in")

            def score_slot(h):
                return slice(0, KEYS) if h % 2 == 0 else slice(3 * 512 - KEYS, 3 * 512)

            def score_cols(h):
                return (0, CACHE) if h % 2 == 0 else (P, 0)

            def prob_chunk(h, c):
                cached, new = score_cols(h)
                at = cached + c * P if c < CCH else new
                return prob[:, h, at:at + P]

            with nc.Block() as block:
                @block.sync
                def _(sp):
                    def step(n, weights, last, finished):
                        if not last:
                            sp.wait_ge(kv_proj, n + 1)
                            sp.nop(nofuse=True)
                            sp.dma_start(x_s[:, :, :].bitcast(F32), xt_dram[bass.ds((n + 1) & 7, 1), :, :, :].rearrange("a p s c -> p (a s) c")).then_inc(x_s_in, 16)
                        if weights:
                            sp.wait_ge(w_split, n + AHEAD)
                            sp.dma_start(w_raw[:, :], w_qkvo[bass.ds(n + AHEAD, 1), :, :].rearrange("a p c -> p (a c)")).then_inc(w_raw_in, 16)
                        if finished:
                            sp.wait_ge(y_added, n)
                            sp.nop(nofuse=True)
                            sp.dma_start(out[bass.ds((n - 1) & 7, 1), :, :].rearrange("a p c -> p (a c)"),
                                         y[:, bass.ds((n - 1) & 7, 1), :].rearrange("p a c -> p (a c)")).then_inc(out_in, 16)

                    sp.dma_start(x_s[:, :, :].bitcast(F32), xt_dram[0:1, :, :, :].rearrange("a p s c -> p (a s) c")).then_inc(x_s_in, 16)
                    with sp.Fori(0, UNITS - AHEAD) as n:
                        step(n, True, False, False)
                    with sp.Fori(UNITS - AHEAD, UNITS - B + 1) as n:
                        step(n, False, False, False)
                    with sp.Fori(UNITS - B + 1, UNITS - 1) as n:
                        step(n, False, False, True)
                    step(UNITS - 1, False, True, True)
                    step(UNITS, False, True, True)
                    sp.wait_ge(out_in, 16 * B)

                @block.gpsimd
                def _(pool):
                    def gather(row, raw, rows, arrived):
                        pool.nop(nofuse=True)
                        nc.gpsimd.indirect_dma_start(
                            raw[:, :], None, rows, bass.IndirectOffsetOnAxis(row[:, 0:1], axis=0)).then_inc(arrived, 16)

                    def next_rows(u):
                        pool.wait_ge(v_in, 16 * u)
                        pool.wait_ge(k_in, 16 * u)
                        pool.nop(nofuse=True)
                        nc.gpsimd.tensor_copy(row_s[:, :], row_id[:, bass.ds(u, 1)]).then_inc(row_set, 1)
                        pool.wait_ge(row_set, u + 1)

                    def rotate(u):
                        pool.wait_ge(var_done, u + 1)
                        nc.gpsimd.tensor_tensor(rstd[:, :], var[:, :], neg_half[:, :], ALU.pow).then_inc(rstd_done, 1)
                        pool.wait_ge(rot_done, u + 1)
                        pool.wait_ge(rot_turned, u)
                        nc.gpsimd.tensor_tensor(rot[:, :, :], rot_a[:, :, :], rot_b[:, :, :], ALU.add).then_inc(rot_sum, 1)

                    def step(n, weights, last):
                        pool.wait_ge(v_in, 16 * (n + 1))
                        pool.wait_ge(pv_done, n)
                        vh = v_hi[:, 0:CCH, :].rearrange("p c d -> p (c d)")
                        vl = v_lo[:, 0:CCH, :].rearrange("p c d -> p (c d)")
                        pool.nop(nofuse=True)
                        nc.gpsimd.tensor_copy(vh, v_raw[:, :]).then_inc(v_round, 1)
                        pool.wait_ge(v_round, n + 1)
                        nc.gpsimd.tensor_tensor(vl, v_raw[:, :], vh.bitcast(F32), ALU.subtract).then_inc(v_split, 1)
                        if not last:
                            pool.wait_ge(v_split, n + 1)
                            gather(row_s, v_raw, v_rows, v_in)
                        for h in range(GROUP):
                            pool.wait_ge(inv_done, GROUP * n + h + 1)
                            pool.nop(nofuse=True)
                            nc.gpsimd.tensor_scalar(prob[:, h, :], prob[:, h, :], inv[:, h:h + 1], None, ALU.mult).then_inc(prob_done, 1)
                        if not last:
                            rotate(n + 1)
                        if weights:
                            pool.wait_ge(q_proj, n + 1)
                            pool.wait_ge(out_proj, n)
                            split_weights(pool, n + AHEAD, w_raw_in, n + 1)
                        if not last:
                            pool.wait_ge(kc_turned, n + 2)

                    next_rows(0)
                    gather(row_s, k_raw, k_rows, k_in)
                    gather(row_s, v_raw, v_rows, v_in)
                    nc.gpsimd.memset(mask[:, 0:P], 0.0).then_inc(blank_set, 1)
                    nc.gpsimd.memset(mask[:, P + CACHE:], 0.0).then_inc(blank_set, 1)
                    rotate(0)
                    pool.wait_ge(kc_turned, 1)
                    next_rows(1)
                    gather(row_s, k_raw, k_rows, k_in)
                    with pool.Fori(0, UNITS - AHEAD) as n:
                        step(n, True, False)
                        next_rows(n + 2)
                        gather(row_s, k_raw, k_rows, k_in)
                    with pool.Fori(UNITS - AHEAD, UNITS - 2) as n:
                        step(n, False, False)
                        next_rows(n + 2)
                        gather(row_s, k_raw, k_rows, k_in)
                    step(UNITS - 2, False, False)
                    step(UNITS - 1, False, True)

                @block.tensor
                def _(pe):
                    def three(dst, lhs, rhs, first, final):
                        (lh, ll), (rh, rl) = lhs, rhs
                        nc.tensor.matmul(dst, lh, rh, start=first, stop=False)
                        nc.tensor.matmul(dst, lh, rl, start=False, stop=False)
                        return nc.tensor.matmul(dst, ll, rh, start=False, stop=final)

                    def weight_rows(unit, at, size):
                        home = ((unit >> 3) & 1) * WCOLS + at
                        return w_hi_flat[:, bass.ds(home, size)], w_lo_flat[:, bass.ds(home, size)]

                    def project(u):
                        pe.wait_ge(x_s_in, 16 * (u + 1))
                        pe.wait_ge(w_split, ((u >> 3) << 3) + B)
                        pe.wait_ge(qt_lo_out, u)
                        nq = GROUP * D
                        for k in range(KT):
                            xs = x_s[:, 0, k * P:(k + 1) * P], x_s[:, 1, k * P:(k + 1) * P]
                            mm = three(ps_q[:, :], xs, weight_rows(u, k * WQKV, nq), k == 0, k == KT - 1)
                        mm.then_inc(q_proj, 1)
                        pe.wait_ge(vn_lo_out, u)
                        for k in range(KT):
                            xs = x_s[:, 0, k * P:(k + 1) * P], x_s[:, 1, k * P:(k + 1) * P]
                            mm = three(ps_kv[:, 0:2 * D], xs, weight_rows(u, k * WQKV + nq, 2 * D), k == 0, k == KT - 1)
                        mm.then_inc(kv_proj, 1)

                    def turn_cached(u):
                        pe.wait_ge(k_in, 16 * (u + 1))
                        for c in range(CCH):
                            mm = nc.tensor.transpose(ps_ring[:, 0, c * P:(c + 1) * P], k_raw[:, c * D:(c + 1) * D], ident[:, :])
                        mm.then_inc(kc_turned, 1)

                    def turn_rotated(u):
                        pe.wait_ge(rot_sum, u + 1)
                        for h in range(GROUP):
                            nc.tensor.transpose(ps_q[:, h * P:(h + 1) * P], rot[:, h, :], ident[:, :])
                        nc.tensor.transpose(ps_kv[:, 2 * D:3 * D], rot[:, GROUP, :], ident[:, :]).then_inc(rot_turned, 1)

                    def score_pair(n, pair):
                        pe.wait_ge(low_done, GROUP * n + 2 * pair)
                        heads = 2 * pair, 2 * pair + 1

                        def part(h, at, size, keys):
                            base = score_slot(h).start + at
                            q = qt_hi[:, h * P:(h + 1) * P], qt_lo[:, h * P:(h + 1) * P]
                            return three(ps_s[:, base:base + size], q, (kt_hi[:, keys], kt_lo[:, keys]), True, True)

                        for h in heads:
                            part(h, score_cols(h)[1], P, slice(CACHE, KEYS))
                        for h in heads:
                            part(h, score_cols(h)[0], CACHE, slice(0, CACHE)).then_inc(scores, 1)

                    def put_out(u):
                        pe.wait_ge(ot_lo_out, u + 1)
                        for h in range(GROUP):
                            ot = ot_hi[:, h * P:(h + 1) * P], ot_lo[:, h * P:(h + 1) * P]
                            mm = three(ps_o[:, :], ot, weight_rows(u, KT * WQKV + h * HID, HID), h == 0, h == GROUP - 1)
                        mm.then_inc(out_proj, 1)

                    def turn_probs(n, c, bank):
                        for h in range(GROUP):
                            if c == 0:
                                pe.wait_ge(prob_done, GROUP * n + h + 1)
                            mm = nc.tensor.transpose(ps_ring[:, bank, h * P:(h + 1) * P], prob_chunk(h, c), ident[:, :])
                        mm.then_inc(p_turned, 1)

                    def values(n, c):
                        pe.wait_ge(pt_lo_out, CH * n + c + 1)
                        mm = three(ps_o[:, :], (v_hi[:, c, :], v_lo[:, c, :]), (pt_hi[:, c, :], pt_lo[:, c, :]),
                                   c == 0, c == CH - 1)
                        if c == CH - 1:
                            mm.then_inc(pv_done, 1)

                    def step(n, last, first=False):
                        pe.wait_ge(qt_lo_out, n + 1)
                        pe.wait_ge(kc_lo_out, n + 1)
                        score_pair(n, 0)
                        if not first:
                            put_out(n - 1)
                        score_pair(n, 1)
                        if not last:
                            project(n + 1)
                        turn_probs(n, 0, 0)
                        if not first:
                            pe.wait_ge(pt_lo_out, CH * n)
                        turn_probs(n, 1, 1)
                        pe.wait_ge(v_split, n + 1)
                        pe.wait_ge(vn_lo_out, n + 1)
                        if not first:
                            pe.wait_ge(y_added, n)
                        values(n, 0)
                        turn_probs(n, 2, 0)
                        values(n, 1)
                        turn_probs(n, 3, 1)
                        values(n, 2)
                        if not last:
                            turn_cached(n + 1)
                        values(n, 3)
                        turn_probs(n, 4, 1)
                        if not last:
                            turn_rotated(n + 1)
                        values(n, 4)

                    project(0)
                    turn_cached(0)
                    turn_rotated(0)
                    step(0, False, first=True)
                    with pe.Fori(1, UNITS - 1) as n:
                        step(n, False)
                    step(UNITS - 1, True)
                    put_out(UNITS - 1)

                @block.scalar
                def _(act):
                    def copy(dst, src):
                        return nc.scalar.activation(dst, src, ACT.Copy)

                    def squares(u):
                        act.wait_ge(q_proj, u + 1)
                        act.wait_ge(var_done, u)
                        for h in range(GROUP + 1):
                            src = ps_q[:, h * D:(h + 1) * D] if h < GROUP else ps_kv[:, 0:D]
                            if h == GROUP:
                                act.wait_ge(kv_proj, u + 1)
                            ins = nc.scalar.activation(junk[:, h, :], src, ACT.Square, accum_out=sq[:, h:h + 1])
                            ins.then_inc(sq_done, 1)

                    def cached_high(u):
                        act.wait_ge(kc_turned, u + 1)
                        act.wait_ge(scores, GROUP * u)
                        copy(kt_hi[:, 0:CACHE], ps_ring[:, 0, :]).then_inc(kc_hi_out, 1)

                    def rotated_high(u):
                        act.wait_ge(rot_turned, u + 1)
                        act.wait_ge(scores, GROUP * u)
                        copy(qt_hi[:, :], ps_q[:, :])
                        copy(kt_hi[:, CACHE:KEYS], ps_kv[:, 2 * D:3 * D]).then_inc(qt_hi_out, 1)

                    def out_high(u):
                        act.wait_ge(pv_done, u + 1)
                        act.wait_ge(out_proj, u)
                        copy(ot_hi[:, :], ps_o[:, :]).then_inc(ot_hi_out, 1)

                    def exps(n, h):
                        act.wait_ge(low_done, GROUP * n + h + 1)
                        act.wait_ge(inv_done, GROUP * n)
                        nc.scalar.activation(prob[:, h, :], prob[:, h, :], ACT.Exp, bias=low[:, h:h + 1], scale=-1.0,
                                             accum_out=total[:, h:h + 1]).then_inc(exp_done, 1)

                    def chunk_high(n, c, bank):
                        act.wait_ge(p_turned, CH * n + c + 1)
                        act.wait_ge(pv_done, n)
                        copy(pt_hi[:, c, :], ps_ring[:, bank, :]).then_inc(pt_hi_out, 1)

                    def step(n, last, first=False):
                        if not first:
                            out_high(n - 1)
                        exps(n, 0)
                        act.wait_ge(kv_proj, n + 1)
                        act.wait_ge(pv_done, n)
                        copy(v_hi[:, CCH, :], ps_kv[:, D:2 * D]).then_inc(vn_hi_out, 1)
                        exps(n, 1)
                        exps(n, 2)
                        exps(n, 3)
                        if not last:
                            squares(n + 1)
                        chunk_high(n, 0, 0)
                        chunk_high(n, 1, 1)
                        chunk_high(n, 2, 0)
                        chunk_high(n, 3, 1)
                        if not last:
                            cached_high(n + 1)
                        chunk_high(n, 4, 1)
                        if not last:
                            rotated_high(n + 1)

                    squares(0)
                    cached_high(0)
                    rotated_high(0)
                    step(0, False, first=True)
                    with act.Fori(1, UNITS - 1) as n:
                        step(n, False)
                    step(UNITS - 1, True)
                    out_high(UNITS - 1)

                @block.vector
                def _(dve):
                    def rest(dst, src, high):
                        return nc.vector.tensor_tensor(dst, src, high.bitcast(F32), ALU.subtract)

                    def set_mask(u):
                        nc.vector.tensor_scalar(mask[:, P:P + CACHE], pos[:, :], len_f[:, bass.ds(u & 7, 1)], NEG,
                                                ALU.is_ge, ALU.mult).then_inc(mask_set, 1)

                    def swap(src, heads):
                        return src.rearrange("p (h s d) -> p h s d", h=heads, s=2)

                    def rotation(u):
                        b = u & 7
                        half = D // 2
                        dve.wait_ge(sq_done, (GROUP + 1) * (u + 1))
                        dve.wait_ge(rstd_done, u)
                        nc.vector.tensor_scalar(var[:, :], sq[:, :], 1.0 / D, EPS, ALU.mult, ALU.add).then_inc(var_done, 1)
                        dve.wait_ge(rot_sum, u)

                        def table(t, lo, hi, heads):
                            return t[:, bass.ds(b, 1), lo:hi].broadcast_to([P, heads, hi - lo])

                        q4 = ps_q[:, :].rearrange("p (h d) -> p h d", h=GROUP)
                        nc.vector.tensor_tensor(rot_a[:, 0:GROUP, :], q4, table(cos_q, 0, D, GROUP), ALU.mult)
                        for o in (0, 1):
                            here = (o * half, (o + 1) * half)
                            nc.vector.tensor_tensor(rot_b[:, 0:GROUP, here[0]:here[1]], q4[:, :, half - here[0]:D - here[0]],
                                                    table(sin_q, *here, GROUP), ALU.mult)
                        dve.wait_ge(rstd_done, u + 1)
                        kr = rstd[:, GROUP:GROUP + 1]
                        k1 = ps_kv[:, 0:D].rearrange("p (h d) -> p h d", h=1)
                        nc.vector.scalar_tensor_tensor(rot_a[:, GROUP:, :], k1, kr, table(cos_k, 0, D, 1), ALU.mult, ALU.mult)
                        for o in (0, 1):
                            here = (o * half, (o + 1) * half)
                            ins = nc.vector.scalar_tensor_tensor(rot_b[:, GROUP:, here[0]:here[1]], k1[:, :, half - here[0]:D - here[0]],
                                                                 kr, table(sin_k, *here, 1), ALU.mult, ALU.mult)
                        ins.then_inc(rot_done, 1)
                        dve.wait_ge(low_done, GROUP * u)
                        nc.vector.tensor_scalar(q_gain[:, :], rstd[:, 0:GROUP], -SCALE, None, ALU.mult).then_inc(gain_done, 1)

                    def cached_low(u):
                        dve.wait_ge(kc_hi_out, u + 1)
                        rest(kt_lo[:, 0:CACHE], ps_ring[:, 0, :], kt_hi[:, 0:CACHE]).then_inc(kc_lo_out, 1)

                    def rotated_low(u):
                        dve.wait_ge(qt_hi_out, u + 1)
                        rest(qt_lo[:, :], ps_q[:, :], qt_hi[:, :])
                        rest(kt_lo[:, CACHE:KEYS], ps_kv[:, 2 * D:3 * D], kt_hi[:, CACHE:KEYS]).then_inc(qt_lo_out, 1)

                    def out_low(u):
                        dve.wait_ge(ot_hi_out, u + 1)
                        rest(ot_lo[:, :], ps_o[:, :], ot_hi[:, :]).then_inc(ot_lo_out, 1)

                    def lowest(n, h):
                        cached, _ = score_cols(h)
                        m = mask[:, P - cached:P - cached + KEYS]
                        dve.wait_ge(scores, GROUP * n + h + 1)
                        dve.nop(nofuse=True)
                        nc.vector.tensor_tensor_reduce(
                            out=prob[:, h, :], in0=ps_s[:, score_slot(h)], in1=m, scale=q_gain[:, h:h + 1], scalar=3.0e38,
                            op0=ALU.add, op1=ALU.min, accum_out=low[:, h:h + 1]).then_inc(low_done, 1)

                    def inverse(n, h):
                        dve.wait_ge(exp_done, GROUP * n + h + 1)
                        nc.vector.reciprocal(inv[:, h:h + 1], total[:, h:h + 1]).then_inc(inv_done, 1)

                    def add_out(u):
                        dve.wait_ge(out_proj, u + 1)
                        yb = y[:, bass.ds(u & 7, 1), :].rearrange("p a c -> p (a c)")
                        nc.vector.tensor_tensor(yb, ps_o[:, :], yb, ALU.add).then_inc(y_added, 1)

                    def chunk_low(n, c, bank):
                        dve.wait_ge(pt_hi_out, CH * n + c + 1)
                        rest(pt_lo[:, c, :], ps_ring[:, bank, :], pt_hi[:, c, :]).then_inc(pt_lo_out, 1)

                    def step(n, last, first=False):
                        if not first:
                            out_low(n - 1)
                        dve.wait_ge(mask_set, n + 1)
                        dve.wait_ge(gain_done, n + 1)
                        dve.wait_ge(p_turned, CH * n)
                        lowest(n, 0)
                        dve.wait_ge(vn_hi_out, n + 1)
                        rest(v_lo[:, CCH, :], ps_kv[:, D:2 * D], v_hi[:, CCH, :]).then_inc(vn_lo_out, 1)
                        lowest(n, 1)
                        inverse(n, 0)
                        if not first:
                            add_out(n - 1)
                        lowest(n, 2)
                        inverse(n, 1)
                        lowest(n, 3)
                        inverse(n, 2)
                        inverse(n, 3)
                        if not last:
                            dve.wait_ge(low_done, GROUP * (n + 1))
                            set_mask(n + 1)
                            rotation(n + 1)
                        chunk_low(n, 0, 0)
                        chunk_low(n, 1, 1)
                        chunk_low(n, 2, 0)
                        chunk_low(n, 3, 1)
                        if not last:
                            cached_low(n + 1)
                        chunk_low(n, 4, 1)
                        if not last:
                            rotated_low(n + 1)

                    dve.wait_ge(blank_set, 2)
                    set_mask(0)
                    rotation(0)
                    cached_low(0)
                    rotated_low(0)
                    step(0, False, first=True)
                    with dve.Fori(1, UNITS - 1) as n:
                        step(n, False)
                    step(UNITS - 1, True)
                    out_low(UNITS - 1)
                    add_out(UNITS - 1)


def kernel(x, itok_B_0_23, itok_B_0_15, itok_B_3_7, itok_Bx16_0_63, itok_B_207_1644, L0_cond_W, L0_cond_b,
           L0_cond_lora_As, L0_cond_lora_Bs, L1_cond_weight, L2_cond_A, L2_cond_B, L3_cond_Wq, L3_cond_Wk,
           L3_cond_Wv, L3_cond_Wo, L3_cond_q_norm_w, L3_cond_k_norm_w, L3_cond_k_cache, L3_cond_v_cache):
    import concourse.bacc as bacc
    from concourse.bass_utils import run_bass_kernel_spmd

    def tiles(a):
        a = np.asarray(a)
        a = a.reshape(*a.shape[:-2], KT, P, a.shape[-1])
        return np.moveaxis(a, -3, -2)

    def swap(a):
        return np.swapaxes(np.asarray(a), -1, -2)

    wq = tiles(swap(L3_cond_Wq)).reshape(P, KT, HK, GROUP * D)
    wk = tiles(swap(L3_cond_Wk)).reshape(P, KT, HK, D)
    wv = tiles(swap(L3_cond_Wv)).reshape(P, KT, HK, D)
    qkv = np.concatenate([wq, wk, wv], axis=3).transpose(2, 0, 1, 3).reshape(HK, P, KT * WQKV)
    wo = swap(L3_cond_Wo).reshape(HK, GROUP, D, HID).transpose(0, 2, 1, 3).reshape(HK, P, GROUP * HID)
    w_qkvo = np.concatenate([qkv, wo], axis=2).reshape(HK, P, B, WCH).transpose(0, 2, 1, 3).reshape(UNITS, P, WCH)

    def cache_rows(a):
        a = np.asarray(a).reshape(PAGES, ROWS_PER_PAGE, CCH, HK, D)
        return a.transpose(3, 0, 1, 2, 4).reshape(HK * PAGES * ROWS_PER_PAGE, CCH * D)

    part = np.arange(P)[:, None]
    unit = np.arange(UNITS)[None, :]
    f32 = np.float32
    inv_freq = (f32(1.0) / f32(THETA) ** (np.arange(0, D, 2, dtype=f32) / f32(D))).astype(f32)
    arrays = {
        "x": np.asarray(x),
        "x_t": tiles(swap(x)).reshape(B, P, HID),
        "ids0": np.asarray(itok_B_0_23).reshape(1, B),
        "ids1": np.asarray(itok_B_0_15).reshape(1, B),
        "ids2": np.asarray(itok_B_3_7).reshape(1, B),
        "table": np.repeat(np.asarray(itok_Bx16_0_63).T, ROWS_PER_PAGE, axis=0),
        "lens": np.asarray(itok_B_207_1644),
        "w0_t": tiles(swap(L0_cond_W)),
        "bias0": np.asarray(L0_cond_b).reshape(1, HID),
        "lora_a": tiles(L0_cond_lora_As),
        "lora_b": np.asarray(L0_cond_lora_Bs),
        "w1_t": tiles(swap(L1_cond_weight)),
        "w2_b": tiles(swap(L2_cond_B)),
        "w2_a": swap(L2_cond_A),
        "w_qkvo": w_qkvo,
        "q_norm": np.asarray(L3_cond_q_norm_w),
        "k_norm": np.asarray(L3_cond_k_norm_w),
        "k_rows": cache_rows(L3_cond_k_cache),
        "v_rows": cache_rows(L3_cond_v_cache),
        "inv_freq": inv_freq,
        "row_in_table": (part % ROWS_PER_PAGE + (unit // B) * PAGES * ROWS_PER_PAGE).astype(np.int32),
        "ident_in": np.eye(P, dtype=f32),
    }
    nc = bacc.Bacc("TRN2", target_bir_lowering=False, num_devices=1)
    sent, args = {}, []
    for name, a in arrays.items():
        a = np.ascontiguousarray(a)
        sent[f"{name}_dram"] = a
        args.append(nc.dram_tensor(f"{name}_dram", a.shape, mybir.dt.from_np(a.dtype), kind="ExternalInput").ap())
    args.append(nc.dram_tensor("out_dram", (B, P, HID), F32, kind="ExternalOutput").ap())
    build(nc, *args)
    r = run_bass_kernel_spmd(nc, [sent], core_ids=[0])
    return r.results[0]["out_dram"]
```

```python
from contextlib import ExitStack

import numpy as np

import concourse.bass as bass
from concourse import mybir

ALU = mybir.AluOpType
ACT = mybir.ActivationFunctionType
F32 = mybir.dt.float32
F32R = mybir.dt.float32r
I32 = mybir.dt.int32

P = 128
B = 8
HID = 512
KT = HID // P
RANK = 16
SLOTS0, SLOTS1, SLOTS2 = 32, 16, 8
HQ, HK, D = 32, 8, 128
GROUP = HQ // HK
PAGES, PSIZE, NPP = 64, 32, 16
CACHE = NPP * PSIZE
CCH = CACHE // P
CH = CCH + 1
KEYS = CACHE + P
ROWS_PER_PAGE = PSIZE // CCH
UNITS = HK * B
WQKV = GROUP * D + 2 * D
WCOLS = KT * WQKV + GROUP * HID
WCH = WCOLS // B
AHEAD = B + 1
THETA = 10000.0
EPS = 1e-06
SCALE = 1.0 / float(np.sqrt(D))
LORA_SCALE = 2.0
NEG = -1e30
TWO_PI = 2.0 * np.pi
TURN_A = 6.28125
TURN_B = float(np.float32(np.round((TWO_PI - TURN_A) * 2.0**21) / 2.0**21))
TURN_C = float(TWO_PI - TURN_A - TURN_B)
ROUND_MAGIC = 1.5 * 2.0**23
PI_BELOW = float(np.nextafter(np.float32(np.pi), np.float32(0.0)))


def build(nc, x, x_t, ids0, ids1, ids2, table, lens, w0_t, bias0, lora_a, lora_b, w1_t, w2_b, w2_a,
          w_qkvo, q_norm, k_norm, k_rows, v_rows, inv_freq, row_in_table, ident_in, out):
    ctx = ExitStack()
    with ctx:
        def sem(name):
            return ctx.enter_context(nc.semaphore(name))

        def sb(name, shape, dt=F32, scope=ctx):
            return scope.enter_context(nc.sbuf_tensor(name, shape, dt))

        def pb(name, shape, scope=ctx):
            return scope.enter_context(nc.psum_tensor(name, shape, F32))

        w_hi = sb("w_hi", [P, 2, WCOLS], F32R)
        w_lo = sb("w_lo", [P, 2, WCOLS], F32R)
        w_raw = sb("w_raw", [P, WCH])
        y = sb("y", [P, B, HID])
        cos_q = sb("cos_q", [P, B, D])
        sin_q = sb("sin_q", [P, B, D])
        cos_k = sb("cos_k", [P, B, D])
        sin_k = sb("sin_k", [P, B, D])
        ident = sb("ident", [P, P])
        pos = sb("pos", [P, CACHE])
        len_f = sb("len_f", [P, B])
        row_id = sb("row_id", [P, UNITS], I32)
        neg_half = sb("neg_half", [P, GROUP + 1])
        xt_dram = nc.dram_tensor("xt_split", [B, P, 2, HID], F32).ap()

        w_first_in = sem("w_first_in")
        w_raw_in = sem("w_raw_in")
        w_split = sem("w_split")
        w_rounded = sem("w_rounded")
        tables_in = sem("tables_in")

        def w_home(chunk):
            return ((chunk >> 3) & 1) * WCOLS + (chunk & 7) * WCH

        w_hi_flat = w_hi[:, :, :].rearrange("p s c -> p (s c)")
        w_lo_flat = w_lo[:, :, :].rearrange("p s c -> p (s c)")

        def weight_high(copy, chunk):
            return copy(w_hi_flat[:, bass.ds(w_home(chunk), WCH)], w_raw[:, :])

        def weight_low(chunk):
            hi = w_hi_flat[:, bass.ds(w_home(chunk), WCH)]
            lo = w_lo_flat[:, bass.ds(w_home(chunk), WCH)]
            return nc.gpsimd.tensor_tensor(lo, w_raw[:, :], hi.bitcast(F32), ALU.subtract)

        with ExitStack() as p1:
            w0 = sb("w0", [P, KT, HID], scope=p1)
            w1 = sb("w1", [P, 2, KT, HID], scope=p1)
            xb = sb("xb", [P, 2, HID], scope=p1)
            xbt = sb("xbt", [P, 2, HID], scope=p1)
            a0 = sb("a0", [P, 2, KT, RANK], scope=p1)
            b0 = sb("b0", [RANK + 1, 2, HID], scope=p1)
            b2 = sb("b2", [P, 2, KT, RANK], scope=p1)
            a2 = sb("a2", [RANK, 2, HID], scope=p1)
            h0 = sb("h0", [RANK + 1, P], scope=p1)
            h2 = sb("h2", [RANK, P], scope=p1)
            x1 = sb("x1", [P, 2, HID], scope=p1)
            x2 = sb("x2", [P, HID], scope=p1)
            x3 = sb("x3", [P, HID], scope=p1)
            x1t = sb("x1t", [P, HID], scope=p1)
            x2t = sb("x2t", [P, HID], scope=p1)
            x3t = sb("x3t", [P, 2, HID], F32R, scope=p1)
            ids = sb("ids", [1, 3, B], I32, scope=p1)
            len_i = sb("len_i", [P, B], I32, scope=p1)
            tab_i = sb("tab_i", [P, B], I32, scope=p1)
            part_row = sb("part_row", [P, UNITS], I32, scope=p1)
            tab8 = sb("tab8", [P, B], I32, scope=p1)
            freq = sb("freq", [P, D // 2], scope=p1)
            wq_row = sb("wq_row", [P, D], scope=p1)
            wk_row = sb("wk_row", [P, D], scope=p1)
            row_f = sb("row_f", [P, B], scope=p1)
            ang = sb("ang", [P, B, D // 2], scope=p1)
            turns = sb("turns", [P, B, D // 2], scope=p1)
            red = sb("red", [P, B, D // 2], scope=p1)
            sin_t = sb("sin_t", [P, B, D // 2], scope=p1)
            cos_t = sb("cos_t", [P, B, D // 2], scope=p1)

            ps_l0 = pb("ps_l0", [P, HID], p1)
            ps_l1 = pb("ps_l1", [P, HID], p1)
            ps_l2 = pb("ps_l2", [P, HID], p1)
            ps_h0 = pb("ps_h0", [P, HID], p1)
            ps_h2 = pb("ps_h2", [P, HID], p1)
            ps_t = pb("ps_t", [P, HID], p1)

            def psem(name):
                return p1.enter_context(nc.semaphore(name))

            w0_in, ids_in = psem("w0_in"), psem("ids_in")
            x_in, xt_in, ab0_in, w1_in, ab2_in = (
                [psem(f"{s}_{slot}") for slot in ("even", "odd")] for s in ("x_in", "xt_in", "ab0_in", "w1_in", "ab2_in"))
            ones_set, pos_set = psem("ones_set"), psem("pos_set")
            h0_done, h0_out, l0_done, x1_out = (psem(s) for s in ("h0_done", "h0_out", "l0_done", "x1_out"))
            t1_done, t1_out, l1_done, x2_out = (psem(s) for s in ("t1_done", "t1_out", "l1_done", "x2_out"))
            t2_done, t2_out, h2_done, h2_out = (psem(s) for s in ("t2_done", "t2_out", "h2_done", "h2_out"))
            l2_done, x3_out, y_out, t3_done = (psem(s) for s in ("l2_done", "x3_out", "y_out", "t3_done"))
            t3_hi, t3_lo, xt_stored = (psem(s) for s in ("t3_hi", "t3_lo", "xt_stored"))
            dve_step, trig_arg, trig_done = (psem(s) for s in ("dve_step", "trig_arg", "trig_done"))
            neg_half_set = psem("neg_half_set")

            with nc.Block() as block:
                @block.sync
                def _(sp):
                    sp.dma_start(ids[:, 0, :], ids0).then_inc(ids_in, 16)
                    sp.dma_start(ids[:, 1, :], ids1).then_inc(ids_in, 16)
                    sp.dma_start(ids[:, 2, :], ids2).then_inc(ids_in, 16)
                    sp.dma_start(w0[:, :, :], w0_t).then_inc(w0_in, 16)
                    for slot in (0, 1):
                        sp.dma_start(b0[RANK:RANK + 1, slot, :], bias0).then_inc(w0_in, 16)
                    sp.wait_ge(ids_in, 48)

                    def load(i, slot, first):
                        b = 2 * i + slot
                        if not first:
                            sp.wait_ge(l0_done, b - 1)
                            sp.nop(nofuse=True)
                        sp.dma_start(xbt[:, slot, :], x_t[bass.ds(b, 1), :, :].rearrange("a p c -> p (a c)")).then_inc(xt_in[slot], 16)
                        id0 = sp.value_load(ids[0:1, 0, bass.ds(b, 1)], min_val=0, max_val=SLOTS0 - 1)
                        sp.dma_start(a0[:, slot, :, :], lora_a[bass.ds(id0, 1), :, :, :].rearrange("a p k r -> p (a k) r")).then_inc(ab0_in[slot], 16)
                        sp.dma_start(b0[0:RANK, slot, :], lora_b[bass.ds(id0, 1), :, :].rearrange("a r c -> (a r) c")).then_inc(ab0_in[slot], 16)
                        if not first:
                            sp.wait_ge(x1_out, b - 1)
                            sp.nop(nofuse=True)
                        sp.dma_start(xb[:, slot, :], x[bass.ds(b, 1), :, :].rearrange("a p c -> p (a c)")).then_inc(x_in[slot], 16)
                        if not first:
                            sp.wait_ge(l1_done, b - 1)
                            sp.nop(nofuse=True)
                        id1 = sp.value_load(ids[0:1, 1, bass.ds(b, 1)], min_val=0, max_val=SLOTS1 - 1)
                        sp.dma_start(w1[:, slot, :, :], w1_t[bass.ds(id1, 1), :, :, :].rearrange("a p k c -> p (a k) c")).then_inc(w1_in[slot], 16)
                        if not first:
                            sp.wait_ge(l2_done, b - 1)
                            sp.nop(nofuse=True)
                        id2 = sp.value_load(ids[0:1, 2, bass.ds(b, 1)], min_val=0, max_val=SLOTS2 - 1)
                        sp.dma_start(b2[:, slot, :, :], w2_b[bass.ds(id2, 1), :, :, :].rearrange("a p k r -> p (a k) r")).then_inc(ab2_in[slot], 16)
                        sp.dma_start(a2[:, slot, :], w2_a[bass.ds(id2, 1), :, :].rearrange("a r c -> (a r) c")).then_inc(ab2_in[slot], 16)

                    load(0, 0, True)
                    load(0, 1, True)
                    with sp.Fori(1, B // 2) as i:
                        load(i, 0, False)
                        load(i, 1, False)

                @block.gpsimd
                def _(pool):
                    nc.gpsimd.iota(pos[:, :], [[1, CCH], [CCH, P]], base=0, channel_multiplier=0,
                                   allow_small_or_imprecise_dtypes=True).then_inc(pos_set, 1)
                    nc.gpsimd.iota(row_f[:, :], [[0, B]], base=0, channel_multiplier=1,
                                   allow_small_or_imprecise_dtypes=True).then_inc(pos_set, 1)
                    nc.gpsimd.memset(neg_half[:, :], -0.5).then_inc(neg_half_set, 1)
                    with pool.Fori(0, AHEAD) as c:
                        pool.dma_start(w_raw[:, :], w_qkvo[bass.ds(c, 1), :, :].rearrange("a p c -> p (a c)")).then_inc(w_first_in, 16)
                        pool.wait_ge(w_first_in, 16 * (c + 1))
                        pool.nop(nofuse=True)
                        weight_high(nc.gpsimd.tensor_copy, c).then_inc(w_rounded, 1)
                        pool.wait_ge(w_rounded, c + 1)
                        weight_low(c).then_inc(w_split, 1)
                        pool.wait_ge(w_split, c + 1)

                @block.scalar
                def _(act):
                    act.dma_start(ident[:, :], ident_in).then_inc(tables_in, 16)
                    act.dma_start(len_i[:, :], lens.partition_broadcast(P)).then_inc(tables_in, 16)
                    act.dma_start(tab_i[:, :], table).then_inc(tables_in, 16)
                    act.dma_start(part_row[:, :], row_in_table).then_inc(tables_in, 16)
                    act.dma_start(freq[:, :], inv_freq.partition_broadcast(P)).then_inc(tables_in, 16)
                    act.dma_start(wq_row[:, :], q_norm.partition_broadcast(P)).then_inc(tables_in, 16)
                    act.dma_start(wk_row[:, :], k_norm.partition_broadcast(P)).then_inc(tables_in, 16)
                    act.wait_ge(trig_arg, 1)
                    nc.scalar.activation(sin_t[:, :, :], red[:, :, :], ACT.Sin).then_inc(trig_done, 1)
                    act.wait_ge(trig_arg, 2)
                    nc.scalar.activation(cos_t[:, :, :], red[:, :, :], ACT.Sin).then_inc(trig_done, 1)

                    def lora_high(b, first=False):
                        act.wait_ge(h0_done, b + 1)
                        if not first:
                            act.wait_ge(l0_done, b)
                        nc.scalar.activation(h0[0:RANK, :], ps_h0[0:RANK, 0:P], ACT.Copy, scale=LORA_SCALE).then_inc(h0_out, 1)

                    def element(b, first=False, last=False):
                        act.wait_ge(t1_done, b + 1)
                        if not first:
                            act.wait_ge(l1_done, b)
                        nc.scalar.activation(x1t[:, :], ps_t[:, :], ACT.Copy).then_inc(t1_out, 1)
                        act.wait_ge(t2_done, b + 1)
                        if not first:
                            act.wait_ge(h2_done, b)
                        nc.scalar.activation(x2t[:, :], ps_t[:, :], ACT.Copy).then_inc(t2_out, 1)
                        if not last:
                            lora_high(b + 1)
                        act.wait_ge(h2_done, b + 1)
                        if not first:
                            act.wait_ge(l2_done, b)
                        nc.scalar.activation(h2[:, :], ps_h2[0:RANK, 0:P], ACT.Copy).then_inc(h2_out, 1)
                        act.wait_ge(t3_done, b + 1)
                        if not first:
                            act.wait_ge(xt_stored, 16 * b)
                        nc.scalar.activation(x3t[:, 0, :], ps_t[:, :], ACT.Copy).then_inc(t3_hi, 1)
                        act.wait_ge(t3_lo, b + 1)
                        act.dma_start(xt_dram[bass.ds(b, 1), :, :, :].rearrange("a p s c -> p (a s) c"), x3t[:, :, :].bitcast(F32)).then_inc(xt_stored, 16)

                    lora_high(0, first=True)
                    element(0, first=True)
                    with act.Fori(1, B - 1) as b:
                        element(b)
                    element(B - 1, last=True)
                    act.wait_ge(xt_stored, 16 * B)

                @block.tensor
                def _(pe):
                    pe.wait_ge(w0_in, 48)
                    pe.wait_ge(tables_in, 16 * 7)
                    pe.wait_ge(ones_set, 1)

                    def turn(src, done):
                        for k in range(KT):
                            mm = nc.tensor.transpose(ps_t[:, k * P:(k + 1) * P], src[:, k * P:(k + 1) * P], ident[:, :])
                        mm.then_inc(done, 1)


                    def lora_in(b, count, slot):
                        pe.wait_ge(ab0_in[slot], 32 * count)
                        for k in range(KT):
                            mm = nc.tensor.matmul(ps_h0[0:RANK, 0:P], a0[:, slot, k, :], xbt[:, slot, k * P:(k + 1) * P],
                                                  start=(k == 0), stop=(k == KT - 1))
                        mm.then_inc(h0_done, 1)

                    def base(b, count, slot, ks):
                        if ks[0] == 0:
                            pe.wait_ge(xt_in[slot], 16 * count)
                        for k in ks:
                            nc.tensor.matmul(ps_l0[:, :], xbt[:, slot, k * P:(k + 1) * P], w0[:, k, :],
                                             start=(k == 0), stop=False)

                    def lora_out(b, slot):
                        pe.wait_ge(h0_out, b + 1)
                        nc.tensor.matmul(ps_l0[:, :], h0[:, :], b0[:, slot, :], start=False, stop=True).then_inc(l0_done, 1)

                    def element(i, slot, first=False, last=False):
                        b = 2 * i + slot
                        other, count = 1 - slot, i + 1 + slot
                        pe.wait_ge(x1_out, b + 1)
                        if not first:
                            pe.wait_ge(t3_lo, b)
                        turn(x1[:, slot, :], t1_done)
                        if not last:
                            base(b + 1, count, other, (0, 1))
                        pe.wait_ge(t1_out, b + 1)
                        pe.wait_ge(w1_in[slot], 16 * (i + 1))
                        for k in range(KT):
                            mm = nc.tensor.matmul(ps_l1[:, :], x1t[:, k * P:(k + 1) * P], w1[:, slot, k, :],
                                                  start=(k == 0), stop=(k == KT - 1))
                        mm.then_inc(l1_done, 1)
                        if not last:
                            base(b + 1, count, other, (2, 3))
                        pe.wait_ge(x2_out, b + 1)
                        turn(x2, t2_done)
                        if not last:
                            lora_in(b + 1, count, other)
                        pe.wait_ge(t2_out, b + 1)
                        pe.wait_ge(ab2_in[slot], 32 * (i + 1))
                        for k in range(KT):
                            mm = nc.tensor.matmul(ps_h2[0:RANK, 0:P], b2[:, slot, k, :], x2t[:, k * P:(k + 1) * P],
                                                  start=(k == 0), stop=(k == KT - 1))
                        mm.then_inc(h2_done, 1)
                        if not last:
                            lora_out(b + 1, other)
                        pe.wait_ge(h2_out, b + 1)
                        nc.tensor.matmul(ps_l2[:, :], h2[:, :], a2[:, slot, :], start=True, stop=True).then_inc(l2_done, 1)
                        pe.wait_ge(x3_out, b + 1)
                        turn(x3, t3_done)

                    base(0, 1, 0, (0, 1, 2, 3))
                    lora_in(0, 1, 0)
                    lora_out(0, 0)
                    element(0, 0, first=True)
                    element(0, 1)
                    with pe.Fori(1, B // 2 - 1) as i:
                        element(i, 0)
                        element(i, 1)
                    element(B // 2 - 1, 0)
                    element(B // 2 - 1, 1, last=True)

                @block.vector
                def _(dve):
                    steps = [0]

                    def step(ins):
                        steps[0] += 1
                        ins.then_inc(dve_step, 1)
                        dve.wait_ge(dve_step, steps[0])

                    nc.vector.memset(h0[:, :], 1.0).then_inc(ones_set, 1)
                    dve.wait_ge(tables_in, 16 * 7)
                    dve.wait_ge(pos_set, 2)
                    step(nc.vector.tensor_copy(len_f[:, :], len_i[:, :]))
                    step(nc.vector.tensor_scalar(tab8[:, :], tab_i[:, :], float(ROWS_PER_PAGE), None, ALU.mult))
                    step(nc.vector.tensor_tensor(
                        row_id[:, :].rearrange("p (g b) -> p g b", g=HK), part_row[:, :].rearrange("p (g b) -> p g b", g=HK),
                        tab8[:, :].rearrange("p (g b) -> p g b", g=1).broadcast_to([P, HK, B]), ALU.add))
                    step(nc.vector.tensor_tensor(row_f[:, :], row_f[:, :], len_f[:, :], ALU.add))
                    step(nc.vector.tensor_tensor(
                        ang[:, :, :], row_f[:, :].rearrange("p (b d) -> p b d", d=1).broadcast_to([P, B, D // 2]),
                        freq[:, :].rearrange("p (b d) -> p b d", b=1).broadcast_to([P, B, D // 2]), ALU.mult))

                    def reduce_angle(quarter):
                        step(nc.vector.tensor_scalar(turns[:, :, :], ang[:, :, :], 1.0 / TWO_PI, 0.25 * quarter, ALU.mult, ALU.add))
                        step(nc.vector.tensor_scalar(turns[:, :, :], turns[:, :, :], ROUND_MAGIC, None, ALU.add))
                        step(nc.vector.tensor_scalar(turns[:, :, :], turns[:, :, :], ROUND_MAGIC, None, ALU.subtract))
                        step(nc.vector.scalar_tensor_tensor(red[:, :, :], turns[:, :, :], -TURN_A, ang[:, :, :], ALU.mult, ALU.add))
                        step(nc.vector.scalar_tensor_tensor(red[:, :, :], turns[:, :, :], -TURN_B, red[:, :, :], ALU.mult, ALU.add))
                        step(nc.vector.scalar_tensor_tensor(red[:, :, :], turns[:, :, :], -TURN_C, red[:, :, :], ALU.mult, ALU.add))
                        step(nc.vector.tensor_scalar(red[:, :, :], red[:, :, :], 0.5 * np.pi * quarter, PI_BELOW, ALU.add, ALU.min))
                        nc.vector.tensor_scalar(red[:, :, :], red[:, :, :], -PI_BELOW, None, ALU.max).then_inc(trig_arg, 1)

                    reduce_angle(0)
                    dve.wait_ge(trig_done, 1)
                    reduce_angle(1)
                    dve.wait_ge(trig_done, 2)
                    half = D // 2
                    for w, cs, sn in ((wq_row, cos_q, sin_q), (wk_row, cos_k, sin_k)):
                        for o in (0, 1):
                            here = slice(o * half, (o + 1) * half)
                            there = slice((1 - o) * half, (2 - o) * half)

                            def wide(s):
                                return w[:, s].rearrange("p (b d) -> p b d", b=1).broadcast_to([P, B, half])

                            nc.vector.tensor_tensor(cs[:, :, here], cos_t[:, :, :], wide(here), ALU.mult)
                            nc.vector.scalar_tensor_tensor(sn[:, :, here], sin_t[:, :, :], -1.0 if o == 0 else 1.0,
                                                           wide(there), ALU.mult, ALU.mult)

                    def first_sum(i, slot):
                        b = 2 * i + slot
                        dve.wait_ge(l0_done, b + 1)
                        dve.wait_ge(x_in[slot], 16 * (i + 1))
                        nc.vector.tensor_tensor(x1[:, slot, :], ps_l0[:, :], xb[:, slot, :], ALU.add).then_inc(x1_out, 1)

                    def element(i, slot, first=False, last=False):
                        b = 2 * i + slot
                        dve.wait_ge(l1_done, b + 1)
                        nc.vector.tensor_tensor(x2[:, :], ps_l1[:, :], x1[:, slot, :], ALU.add).then_inc(x2_out, 1)
                        if not last:
                            first_sum(i + slot, 1 - slot)
                        dve.wait_ge(l2_done, b + 1)
                        dve.wait_ge(x2_out, b + 1)
                        if not first:
                            dve.wait_ge(y_out, b)
                        nc.vector.tensor_tensor(x3[:, :], ps_l2[:, :], x2[:, :], ALU.add).then_inc(x3_out, 1)
                        dve.wait_ge(x3_out, b + 1)
                        nc.vector.tensor_copy(y[:, bass.ds(b, 1), :].rearrange("p a c -> p (a c)"), x3[:, :]).then_inc(y_out, 1)
                        dve.wait_ge(t3_hi, b + 1)
                        nc.vector.tensor_tensor(x3t[:, 1, :], ps_t[:, :], x3t[:, 0, :].bitcast(F32), ALU.subtract).then_inc(t3_lo, 1)

                    first_sum(0, 0)
                    element(0, 0, first=True)
                    element(0, 1)
                    with dve.Fori(1, B // 2 - 1) as i:
                        element(i, 0)
                        element(i, 1)
                    element(B // 2 - 1, 0)
                    element(B // 2 - 1, 1, last=True)

        with ExitStack() as p2:
            x_s = sb("x_s", [P, 2, HID], F32R, scope=p2)
            k_raw = sb("k_raw", [P, CCH * D], scope=p2)
            v_raw = sb("v_raw", [P, CCH * D], scope=p2)
            row_s = sb("row_s", [P, 1], I32, scope=p2)
            kt_hi = sb("kt_hi", [P, KEYS], F32R, scope=p2)
            kt_lo = sb("kt_lo", [P, KEYS], F32R, scope=p2)
            v_hi = sb("v_hi", [P, CH, D], F32R, scope=p2)
            v_lo = sb("v_lo", [P, CH, D], F32R, scope=p2)
            qt_hi = sb("qt_hi", [P, GROUP * P], F32R, scope=p2)
            qt_lo = sb("qt_lo", [P, GROUP * P], F32R, scope=p2)
            prob = sb("prob", [P, GROUP, KEYS], scope=p2)
            pt_hi = sb("pt_hi", [P, CH, GROUP * P], F32R, scope=p2)
            pt_lo = sb("pt_lo", [P, CH, GROUP * P], F32R, scope=p2)
            ot_hi = sb("ot_hi", [P, GROUP * P], F32R, scope=p2)
            ot_lo = sb("ot_lo", [P, GROUP * P], F32R, scope=p2)
            rot_a = sb("rot_a", [P, GROUP + 1, D], scope=p2)
            rot_b = sb("rot_b", [P, GROUP + 1, D], scope=p2)
            rot = sb("rot", [P, GROUP + 1, D], scope=p2)
            key_sum = sb("key_sum", [P, D], scope=p2)
            mask = sb("mask", [P, KEYS], scope=p2)
            junk = sb("junk", [P, GROUP + 1, D], scope=p2)
            sq = sb("sq", [P, GROUP + 1], scope=p2)
            var = sb("var", [P, GROUP + 1], scope=p2)
            rstd = sb("rstd", [P, GROUP + 1], scope=p2)
            q_gain = sb("q_gain", [P, GROUP], scope=p2)
            low = sb("low", [P, GROUP], scope=p2)
            total = sb("total", [P, GROUP], scope=p2)
            inv = sb("inv", [P, GROUP], scope=p2)

            ps_s = pb("ps_s", [P, 3 * 512], p2)
            ps_ring = pb("ps_ring", [P, 2, 512], p2)
            ps_q = pb("ps_q", [P, 512], p2)
            ps_kv = pb("ps_kv", [P, 512], p2)
            ps_o = pb("ps_o", [P, 512], p2)

            def psem(name):
                return p2.enter_context(nc.semaphore(name))

            x_s_in, k_in, v_in = psem("x_s_in"), psem("k_in"), psem("v_in")
            row_set, mask_set, blank_set = psem("row_set"), psem("mask_set"), psem("blank_set")
            q_proj, kv_proj = psem("q_proj"), psem("kv_proj")
            sq_done, var_done, rstd_done, gain_done = (psem(s) for s in ("sq_done", "var_done", "rstd_done", "gain_done"))
            key_rotated = psem("key_rotated")
            q_rotated, q_summed, key_summed, key_scaled, rot_turned = (
                psem(s) for s in ("q_rotated", "q_summed", "key_summed", "key_scaled", "rot_turned"))
            qt_hi_out, qt_lo_out = psem("qt_hi_out"), psem("qt_lo_out")
            kc_turned, kc_hi_out, kc_lo_out = psem("kc_turned"), psem("kc_hi_out"), psem("kc_lo_out")
            v_hi_out, v_split, vn_hi_out, vn_lo_out = (psem(s) for s in ("v_round", "v_split", "vn_hi_out", "vn_lo_out"))
            scores, low_done, exp_done, inv_done, prob_done = (psem(s) for s in ("scores", "low_done", "exp_done", "inv_done", "prob_done"))
            p_turned, pt_hi_out, pt_lo_out = psem("p_turned"), psem("pt_hi_out"), psem("pt_lo_out")
            pv_done, ot_hi_out, ot_lo_out = psem("pv_done"), psem("ot_hi_out"), psem("ot_lo_out")
            out_proj, y_added, out_in = psem("out_proj"), psem("y_added"), psem("out_in")

            MIDDLE = KEYS - (512 - P)
            CUTS = ((KEYS - MIDDLE, KEYS), (0, KEYS - MIDDLE)), ((0, MIDDLE), (MIDDLE, KEYS))

            def score_slot(h):
                return P + (h % 2) * KEYS

            with nc.Block() as block:
                @block.sync
                def _(sp):
                    def step(n, weights, last, finished):
                        if not last:
                            sp.wait_ge(kv_proj, n + 1)
                            sp.nop(nofuse=True)
                            sp.dma_start(x_s[:, :, :].bitcast(F32), xt_dram[bass.ds((n + 1) & 7, 1), :, :, :].rearrange("a p s c -> p (a s) c")).then_inc(x_s_in, 16)
                        if weights:
                            sp.wait_ge(w_split, n + AHEAD)
                            sp.dma_start(w_raw[:, :], w_qkvo[bass.ds(n + AHEAD, 1), :, :].rearrange("a p c -> p (a c)")).then_inc(w_raw_in, 16)
                        if finished:
                            sp.wait_ge(y_added, n)
                            sp.nop(nofuse=True)
                            sp.dma_start(out[bass.ds((n - 1) & 7, 1), :, :].rearrange("a p c -> p (a c)"),
                                         y[:, bass.ds((n - 1) & 7, 1), :].rearrange("p a c -> p (a c)")).then_inc(out_in, 16)

                    sp.dma_start(x_s[:, :, :].bitcast(F32), xt_dram[0:1, :, :, :].rearrange("a p s c -> p (a s) c")).then_inc(x_s_in, 16)
                    with sp.Fori(0, UNITS - AHEAD) as n:
                        step(n, True, False, False)
                    with sp.Fori(UNITS - AHEAD, UNITS - B + 1) as n:
                        step(n, False, False, False)
                    with sp.Fori(UNITS - B + 1, UNITS - 1) as n:
                        step(n, False, False, True)
                    step(UNITS - 1, False, True, True)
                    step(UNITS, False, True, True)
                    sp.wait_ge(out_in, 16 * B)

                @block.gpsimd
                def _(pool):
                    def gather(row, raw, rows, arrived):
                        pool.nop(nofuse=True)
                        nc.gpsimd.indirect_dma_start(
                            raw[:, :], None, rows, bass.IndirectOffsetOnAxis(row[:, 0:1], axis=0)).then_inc(arrived, 16)

                    def next_rows(u, first=False):
                        if not first:
                            pool.wait_ge(v_in, 16 * u)
                            pool.wait_ge(k_in, 16 * u)
                        pool.nop(nofuse=True)
                        nc.gpsimd.tensor_copy(row_s[:, :], row_id[:, bass.ds(u, 1)]).then_inc(row_set, 1)
                        pool.wait_ge(row_set, u + 1)

                    def next_keys(u):
                        pool.wait_ge(kc_turned, u)
                        next_rows(u)
                        gather(row_s, k_raw, k_rows, k_in)

                    def sum_queries(u, first=False):
                        pool.wait_ge(q_rotated, u + 1)
                        if not first:
                            pool.wait_ge(rot_turned, u)
                        nc.gpsimd.tensor_tensor(rot[:, 0:GROUP, :], rot_a[:, 0:GROUP, :], rot_b[:, 0:GROUP, :], ALU.add).then_inc(q_summed, 1)

                    def norm_factors(u):
                        pool.wait_ge(var_done, u + 1)
                        nc.gpsimd.tensor_tensor(rstd[:, :], var[:, :], neg_half[:, :], ALU.pow).then_inc(rstd_done, 1)

                    def step(n, weights, last, first=False):
                        vl = v_lo[:, 0:CCH, :].rearrange("p c d -> p (c d)")
                        vh = v_hi[:, 0:CCH, :].rearrange("p c d -> p (c d)")
                        pool.wait_ge(v_hi_out, n + 1)
                        nc.gpsimd.tensor_tensor(vl, v_raw[:, :], vh.bitcast(F32), ALU.subtract).then_inc(v_split, 1)
                        if not last:
                            pool.wait_ge(v_split, n + 1)
                            gather(row_s, v_raw, v_rows, v_in)
                        if weights:
                            pool.wait_ge(w_rounded, n + AHEAD + 1)
                            weight_low(n + AHEAD).then_inc(w_split, 1)
                        if not last:
                            sum_queries(n + 1)
                            norm_factors(n + 1)

                    next_rows(0, first=True)
                    gather(row_s, k_raw, k_rows, k_in)
                    gather(row_s, v_raw, v_rows, v_in)
                    nc.gpsimd.memset(mask[:, CACHE:], 0.0).then_inc(blank_set, 1)
                    sum_queries(0, first=True)
                    norm_factors(0)
                    next_keys(1)
                    with pool.Fori(0, UNITS - AHEAD) as n:
                        step(n, True, False)
                        next_keys(n + 2)
                    with pool.Fori(UNITS - AHEAD, UNITS - 2) as n:
                        step(n, False, False)
                        next_keys(n + 2)
                    step(UNITS - 2, False, False)
                    step(UNITS - 1, False, True)

                @block.tensor
                def _(pe):
                    def three(dst, lhs, rhs, first, final):
                        (lh, ll), (rh, rl) = lhs, rhs
                        nc.tensor.matmul(dst, lh, rh, start=first, stop=False)
                        nc.tensor.matmul(dst, lh, rl, start=False, stop=False)
                        return nc.tensor.matmul(dst, ll, rh, start=False, stop=final)

                    def weight_rows(unit, at, size):
                        home = ((unit >> 3) & 1) * WCOLS + at
                        return w_hi_flat[:, bass.ds(home, size)], w_lo_flat[:, bass.ds(home, size)]

                    def project(dst, u, at, size, ks=range(KT)):
                        for k in ks:
                            xs = x_s[:, 0, k * P:(k + 1) * P], x_s[:, 1, k * P:(k + 1) * P]
                            mm = three(dst, xs, weight_rows(u, k * WQKV + at, size), k == 0, k == KT - 1)
                        return mm

                    def project_queries(u, first=False):
                        pe.wait_ge(x_s_in, 16 * (u + 1))
                        if not first:
                            pe.wait_ge(w_split, ((u >> 3) << 3) + B)
                            pe.wait_ge(qt_lo_out, u)
                        project(ps_q[:, :], u, 0, GROUP * D, (0, 1))

                    def project_queries_rest(u):
                        project(ps_q[:, :], u, 0, GROUP * D, (2, 3)).then_inc(q_proj, 1)

                    def project_new_key(u, first=False):
                        if not first:
                            pe.wait_ge(vn_lo_out, u)
                        project(ps_kv[:, 0:2 * D], u, GROUP * D, 2 * D).then_inc(kv_proj, 1)

                    def turn_cached(u):
                        pe.wait_ge(k_in, 16 * (u + 1))
                        for c in range(CCH):
                            mm = nc.tensor.transpose(ps_ring[:, 0, c * P:(c + 1) * P], k_raw[:, c * D:(c + 1) * D], ident[:, :])
                        mm.then_inc(kc_turned, 1)

                    def turn_rotated(u):
                        pe.wait_ge(q_summed, u + 1)
                        pe.wait_ge(key_scaled, u + 1)
                        for h in range(GROUP):
                            nc.tensor.transpose(ps_q[:, h * P:(h + 1) * P], rot[:, h, :], ident[:, :])
                        nc.tensor.transpose(ps_kv[:, 2 * D:3 * D], rot[:, GROUP, :], ident[:, :]).then_inc(rot_turned, 1)

                    def score_pair(n, pair):
                        pe.wait_ge(low_done, GROUP * n + 2 * pair)
                        heads = 2 * pair, 2 * pair + 1

                        def part(h, piece):
                            lo, hi = CUTS[h % 2][piece]
                            q = qt_hi[:, h * P:(h + 1) * P], qt_lo[:, h * P:(h + 1) * P]
                            return three(ps_s[:, score_slot(h) + lo:score_slot(h) + hi], q,
                                         (kt_hi[:, lo:hi], kt_lo[:, lo:hi]), True, True)

                        for h in heads:
                            part(h, 0)
                        for h in heads:
                            part(h, 1).then_inc(scores, 1)

                    def put_out(u):
                        pe.wait_ge(ot_lo_out, u + 1)
                        for h in range(GROUP):
                            ot = ot_hi[:, h * P:(h + 1) * P], ot_lo[:, h * P:(h + 1) * P]
                            mm = three(ps_o[:, :], ot, weight_rows(u, KT * WQKV + h * HID, HID), h == 0, h == GROUP - 1)
                        mm.then_inc(out_proj, 1)

                    def turn_probs(n, c, bank):
                        for h in range(GROUP):
                            if c == 0:
                                pe.wait_ge(prob_done, GROUP * n + h + 1)
                            mm = nc.tensor.transpose(ps_ring[:, bank, h * P:(h + 1) * P], prob[:, h, c * P:(c + 1) * P], ident[:, :])
                        mm.then_inc(p_turned, 1)

                    def values(n, c):
                        pe.wait_ge(pt_lo_out, CH * n + c + 1)
                        mm = three(ps_o[:, :], (v_hi[:, c, :], v_lo[:, c, :]), (pt_hi[:, c, :], pt_lo[:, c, :]),
                                   c == 0, c == CH - 1)
                        if c == CH - 1:
                            mm.then_inc(pv_done, 1)

                    def step(n, last, first=False):
                        pe.wait_ge(qt_lo_out, n + 1)
                        pe.wait_ge(kc_lo_out, n + 1)
                        score_pair(n, 0)
                        if not last:
                            project_queries(n + 1)
                        score_pair(n, 1)
                        if not last:
                            turn_cached(n + 1)
                        if not first:
                            put_out(n - 1)
                        if not last:
                            project_queries_rest(n + 1)
                        turn_probs(n, 0, 1)
                        pe.wait_ge(kc_lo_out, n + 1 if last else n + 2)
                        turn_probs(n, 1, 0)
                        if not last:
                            project_new_key(n + 1)
                        pe.wait_ge(v_split, n + 1)
                        pe.wait_ge(vn_lo_out, n + 1)
                        if not first:
                            pe.wait_ge(y_added, n)
                        values(n, 0)
                        turn_probs(n, 2, 1)
                        values(n, 1)
                        turn_probs(n, 3, 0)
                        if not last:
                            turn_rotated(n + 1)
                        pe.wait_ge(pt_lo_out, CH * n + 3)
                        turn_probs(n, 4, 1)
                        values(n, 2)
                        values(n, 3)
                        values(n, 4)

                    project_queries(0, first=True)
                    project_queries_rest(0)
                    project_new_key(0, first=True)
                    turn_cached(0)
                    turn_rotated(0)
                    step(0, False, first=True)
                    with pe.Fori(1, UNITS - 1) as n:
                        step(n, False)
                    step(UNITS - 1, True)
                    put_out(UNITS - 1)

                @block.scalar
                def _(act):
                    def copy(dst, src):
                        return nc.scalar.activation(dst, src, ACT.Copy)

                    def square(src, h):
                        nc.scalar.activation(junk[:, h, :], src, ACT.Square, accum_out=sq[:, h:h + 1]).then_inc(sq_done, 1)

                    def query_squares(u, first=False):
                        act.wait_ge(q_rotated, u + 1)
                        if not first:
                            act.wait_ge(var_done, u)
                        for h in range(GROUP):
                            square(ps_q[:, h * D:(h + 1) * D], h)

                    def key_squares(u):
                        act.wait_ge(kv_proj, u + 1)
                        square(ps_kv[:, 0:D], GROUP)

                    def scale_key(u):
                        act.wait_ge(key_summed, u + 1)
                        act.wait_ge(rstd_done, u + 1)
                        nc.scalar.activation(rot[:, GROUP, :], key_sum[:, :], ACT.Copy, scale=rstd[:, GROUP:GROUP + 1]).then_inc(key_scaled, 1)

                    def cached_high(u, first=False):
                        act.wait_ge(kc_turned, u + 1)
                        if not first:
                            act.wait_ge(scores, GROUP * u)
                        copy(kt_hi[:, 0:CACHE], ps_ring[:, 0, :]).then_inc(kc_hi_out, 1)

                    def rotated_high(u):
                        act.wait_ge(rot_turned, u + 1)
                        copy(qt_hi[:, :], ps_q[:, :])
                        copy(kt_hi[:, CACHE:KEYS], ps_kv[:, 2 * D:3 * D]).then_inc(qt_hi_out, 1)

                    def out_high(u):
                        act.wait_ge(pv_done, u + 1)
                        copy(ot_hi[:, :], ps_o[:, :]).then_inc(ot_hi_out, 1)

                    def exps(n, h):
                        act.wait_ge(low_done, GROUP * n + h + 1)
                        nc.scalar.activation(prob[:, h, :], prob[:, h, :], ACT.Exp, bias=low[:, h:h + 1], scale=-1.0,
                                             accum_out=total[:, h:h + 1]).then_inc(exp_done, 1)

                    def normalize(n, h):
                        act.wait_ge(inv_done, GROUP * n + h + 1)
                        nc.scalar.activation(prob[:, h, :], prob[:, h, :], ACT.Copy, scale=inv[:, h:h + 1]).then_inc(prob_done, 1)

                    def chunk_high(n, c, bank):
                        act.wait_ge(p_turned, CH * n + c + 1)
                        copy(pt_hi[:, c, :], ps_ring[:, bank, :]).then_inc(pt_hi_out, 1)

                    def step(n, last, first=False):
                        if not first:
                            out_high(n - 1)
                        exps(n, 0)
                        exps(n, 1)
                        act.wait_ge(kv_proj, n + 1)
                        copy(v_hi[:, CCH, :], ps_kv[:, D:2 * D]).then_inc(vn_hi_out, 1)
                        normalize(n, 0)
                        normalize(n, 1)
                        exps(n, 2)
                        exps(n, 3)
                        if not last:
                            cached_high(n + 1)
                        normalize(n, 2)
                        normalize(n, 3)
                        chunk_high(n, 0, 1)
                        chunk_high(n, 1, 0)
                        if not last:
                            query_squares(n + 1)
                            key_squares(n + 1)
                        chunk_high(n, 2, 1)
                        if not last:
                            scale_key(n + 1)
                        chunk_high(n, 3, 0)
                        chunk_high(n, 4, 1)
                        if not last:
                            rotated_high(n + 1)

                    query_squares(0, first=True)
                    key_squares(0)
                    scale_key(0)
                    cached_high(0, first=True)
                    rotated_high(0)
                    step(0, False, first=True)
                    with act.Fori(1, UNITS - 1) as n:
                        step(n, False)
                    step(UNITS - 1, True)
                    out_high(UNITS - 1)

                @block.vector
                def _(dve):
                    def rest(dst, src, high):
                        return nc.vector.tensor_tensor(dst, src, high.bitcast(F32), ALU.subtract)

                    def set_mask(u):
                        nc.vector.tensor_scalar(mask[:, 0:CACHE], pos[:, :], len_f[:, bass.ds(u & 7, 1)], NEG,
                                                ALU.is_ge, ALU.mult).then_inc(mask_set, 1)

                    def swap(src, heads):
                        return src.rearrange("p (h s d) -> p h s d", h=heads, s=2)

                    def halves(u, table, heads):
                        for o in (0, D // 2):
                            yield slice(o, o + D // 2), slice(D // 2 - o, D - o), table[:, bass.ds(u & 7, 1), o:o + D // 2].broadcast_to([P, heads, D // 2])

                    def rotate_queries(u, first=False):
                        dve.wait_ge(q_proj, u + 1)
                        if not first:
                            dve.wait_ge(q_summed, u)
                        q = ps_q[:, :].rearrange("p (h d) -> p h d", h=GROUP)
                        nc.vector.tensor_tensor(rot_a[:, 0:GROUP, :], q, cos_q[:, bass.ds(u & 7, 1), :].broadcast_to([P, GROUP, D]), ALU.mult)
                        for here, there, sines in halves(u, sin_q, GROUP):
                            ins = nc.vector.tensor_tensor(rot_b[:, 0:GROUP, here], q[:, :, there], sines, ALU.mult)
                        ins.then_inc(q_rotated, 1)

                    def variances(u, first=False):
                        dve.wait_ge(sq_done, (GROUP + 1) * (u + 1))
                        if not first:
                            dve.wait_ge(rstd_done, u)
                        nc.vector.tensor_scalar(var[:, :], sq[:, :], 1.0 / D, EPS, ALU.mult, ALU.add).then_inc(var_done, 1)

                    def rotate_key(u, first=False):
                        if not first:
                            dve.wait_ge(key_scaled, u)
                        key = ps_kv[:, 0:D].rearrange("p (h d) -> p h d", h=1)
                        nc.vector.tensor_tensor(rot_a[:, GROUP:, :], key, cos_k[:, bass.ds(u & 7, 1), :], ALU.mult)
                        for here, there, sines in halves(u, sin_k, 1):
                            ins = nc.vector.tensor_tensor(rot_b[:, GROUP:, here], key[:, :, there], sines, ALU.mult)
                        ins.then_inc(key_rotated, 1)
                        dve.wait_ge(key_rotated, u + 1)
                        nc.vector.tensor_tensor(key_sum[:, :], rot_a[:, GROUP, :], rot_b[:, GROUP, :], ALU.add).then_inc(key_summed, 1)

                    def gains(u, first=False):
                        dve.wait_ge(rstd_done, u + 1)
                        nc.vector.tensor_scalar(q_gain[:, :], rstd[:, 0:GROUP], -SCALE, None, ALU.mult).then_inc(gain_done, 1)

                    def values_high(n, first=False):
                        dve.wait_ge(v_in, 16 * (n + 1))
                        if not first:
                            dve.wait_ge(pv_done, n)
                        nc.vector.tensor_copy(v_hi[:, 0:CCH, :].rearrange("p c d -> p (c d)"), v_raw[:, :]).then_inc(v_hi_out, 1)

                    def weights_high(n):
                        dve.wait_ge(w_raw_in, 16 * (n + 1))
                        weight_high(nc.vector.tensor_copy, n + AHEAD).then_inc(w_rounded, 1)

                    def cached_low(u):
                        dve.wait_ge(kc_hi_out, u + 1)
                        rest(kt_lo[:, 0:CACHE], ps_ring[:, 0, :], kt_hi[:, 0:CACHE]).then_inc(kc_lo_out, 1)

                    def rotated_low(u):
                        dve.wait_ge(qt_hi_out, u + 1)
                        rest(qt_lo[:, :], ps_q[:, :], qt_hi[:, :])
                        rest(kt_lo[:, CACHE:KEYS], ps_kv[:, 2 * D:3 * D], kt_hi[:, CACHE:KEYS]).then_inc(qt_lo_out, 1)

                    def out_low(u):
                        dve.wait_ge(ot_hi_out, u + 1)
                        rest(ot_lo[:, :], ps_o[:, :], ot_hi[:, :]).then_inc(ot_lo_out, 1)

                    def lowest(n, h):
                        dve.wait_ge(scores, GROUP * n + h + 1)
                        dve.nop(nofuse=True)
                        nc.vector.tensor_tensor_reduce(
                            out=prob[:, h, :], in0=ps_s[:, score_slot(h):score_slot(h) + KEYS], in1=mask[:, :], scale=q_gain[:, h:h + 1], scalar=3.0e38,
                            op0=ALU.add, op1=ALU.min, accum_out=low[:, h:h + 1]).then_inc(low_done, 1)

                    def inverse(n, h):
                        dve.wait_ge(exp_done, GROUP * n + h + 1)
                        nc.vector.reciprocal(inv[:, h:h + 1], total[:, h:h + 1]).then_inc(inv_done, 1)

                    def add_out(u):
                        dve.wait_ge(out_proj, u + 1)
                        yb = y[:, bass.ds(u & 7, 1), :].rearrange("p a c -> p (a c)")
                        nc.vector.tensor_tensor(yb, ps_o[:, :], yb, ALU.add).then_inc(y_added, 1)

                    def chunk_low(n, c, bank):
                        dve.wait_ge(pt_hi_out, CH * n + c + 1)
                        rest(pt_lo[:, c, :], ps_ring[:, bank, :], pt_hi[:, c, :]).then_inc(pt_lo_out, 1)

                    def step(n, weights, last, first=False):
                        if not first:
                            out_low(n - 1)
                        dve.wait_ge(mask_set, n + 1)
                        dve.wait_ge(gain_done, n + 1)
                        if not first:
                            dve.wait_ge(p_turned, CH * n)
                        lowest(n, 0)
                        lowest(n, 1)
                        inverse(n, 0)
                        values_high(n, first)
                        inverse(n, 1)
                        dve.wait_ge(vn_hi_out, n + 1)
                        rest(v_lo[:, CCH, :], ps_kv[:, D:2 * D], v_hi[:, CCH, :]).then_inc(vn_lo_out, 1)
                        if weights:
                            weights_high(n)
                        lowest(n, 2)
                        lowest(n, 3)
                        if not last:
                            dve.wait_ge(low_done, GROUP * (n + 1))
                            set_mask(n + 1)
                        inverse(n, 2)
                        inverse(n, 3)
                        if not last:
                            cached_low(n + 1)
                        if not first:
                            add_out(n - 1)
                        if not last:
                            rotate_queries(n + 1)
                        chunk_low(n, 0, 1)
                        chunk_low(n, 1, 0)
                        if not last:
                            variances(n + 1)
                            rotate_key(n + 1)
                        chunk_low(n, 2, 1)
                        chunk_low(n, 3, 0)
                        chunk_low(n, 4, 1)
                        if not last:
                            gains(n + 1)
                            rotated_low(n + 1)

                    dve.wait_ge(blank_set, 1)
                    set_mask(0)
                    rotate_queries(0, first=True)
                    variances(0, first=True)
                    rotate_key(0, first=True)
                    gains(0)
                    cached_low(0)
                    rotated_low(0)
                    step(0, True, False, first=True)
                    with dve.Fori(1, UNITS - AHEAD) as n:
                        step(n, True, False)
                    with dve.Fori(UNITS - AHEAD, UNITS - 1) as n:
                        step(n, False, False)
                    step(UNITS - 1, False, True)
                    out_low(UNITS - 1)
                    add_out(UNITS - 1)


def kernel(x, itok_B_0_23, itok_B_0_15, itok_B_3_7, itok_Bx16_0_63, itok_B_207_1644, L0_cond_W, L0_cond_b,
           L0_cond_lora_As, L0_cond_lora_Bs, L1_cond_weight, L2_cond_A, L2_cond_B, L3_cond_Wq, L3_cond_Wk,
           L3_cond_Wv, L3_cond_Wo, L3_cond_q_norm_w, L3_cond_k_norm_w, L3_cond_k_cache, L3_cond_v_cache):
    import concourse.bacc as bacc
    from concourse.bass_utils import run_bass_kernel_spmd

    def tiles(a):
        a = np.asarray(a)
        a = a.reshape(*a.shape[:-2], KT, P, a.shape[-1])
        return np.moveaxis(a, -3, -2)

    def swap(a):
        return np.swapaxes(np.asarray(a), -1, -2)

    wq = tiles(swap(L3_cond_Wq)).reshape(P, KT, HK, GROUP * D)
    wk = tiles(swap(L3_cond_Wk)).reshape(P, KT, HK, D)
    wv = tiles(swap(L3_cond_Wv)).reshape(P, KT, HK, D)
    qkv = np.concatenate([wq, wk, wv], axis=3).transpose(2, 0, 1, 3).reshape(HK, P, KT * WQKV)
    wo = swap(L3_cond_Wo).reshape(HK, GROUP, D, HID).transpose(0, 2, 1, 3).reshape(HK, P, GROUP * HID)
    w_qkvo = np.concatenate([qkv, wo], axis=2).reshape(HK, P, B, WCH).transpose(0, 2, 1, 3).reshape(UNITS, P, WCH)

    def cache_rows(a):
        a = np.asarray(a).reshape(PAGES, ROWS_PER_PAGE, CCH, HK, D)
        return a.transpose(3, 0, 1, 2, 4).reshape(HK * PAGES * ROWS_PER_PAGE, CCH * D)

    part = np.arange(P)[:, None]
    unit = np.arange(UNITS)[None, :]
    f32 = np.float32
    inv_freq = (f32(1.0) / f32(THETA) ** (np.arange(0, D, 2, dtype=f32) / f32(D))).astype(f32)
    arrays = {
        "x": np.asarray(x),
        "x_t": tiles(swap(x)).reshape(B, P, HID),
        "ids0": np.asarray(itok_B_0_23).reshape(1, B),
        "ids1": np.asarray(itok_B_0_15).reshape(1, B),
        "ids2": np.asarray(itok_B_3_7).reshape(1, B),
        "table": np.repeat(np.asarray(itok_Bx16_0_63).T, ROWS_PER_PAGE, axis=0),
        "lens": np.asarray(itok_B_207_1644),
        "w0_t": tiles(swap(L0_cond_W)),
        "bias0": np.asarray(L0_cond_b).reshape(1, HID),
        "lora_a": tiles(L0_cond_lora_As),
        "lora_b": np.asarray(L0_cond_lora_Bs),
        "w1_t": tiles(swap(L1_cond_weight)),
        "w2_b": tiles(swap(L2_cond_B)),
        "w2_a": swap(L2_cond_A),
        "w_qkvo": w_qkvo,
        "q_norm": np.asarray(L3_cond_q_norm_w),
        "k_norm": np.asarray(L3_cond_k_norm_w),
        "k_rows": cache_rows(L3_cond_k_cache),
        "v_rows": cache_rows(L3_cond_v_cache),
        "inv_freq": inv_freq,
        "row_in_table": (part % ROWS_PER_PAGE + (unit // B) * PAGES * ROWS_PER_PAGE).astype(np.int32),
        "ident_in": np.eye(P, dtype=f32),
    }
    nc = bacc.Bacc("TRN2", target_bir_lowering=False, num_devices=1)
    sent, args = {}, []
    for name, a in arrays.items():
        a = np.ascontiguousarray(a)
        sent[f"{name}_dram"] = a
        args.append(nc.dram_tensor(f"{name}_dram", a.shape, mybir.dt.from_np(a.dtype), kind="ExternalInput").ap())
    args.append(nc.dram_tensor("out_dram", (B, P, HID), F32, kind="ExternalOutput").ap())
    build(nc, *args)
    r = run_bass_kernel_spmd(nc, [sent], core_ids=[0])
    return r.results[0]["out_dram"]
```

```python
from contextlib import ExitStack

import numpy as np

import concourse.bass as bass
from concourse import mybir

ALU = mybir.AluOpType
ACT = mybir.ActivationFunctionType
F32 = mybir.dt.float32
F32R = mybir.dt.float32r
I32 = mybir.dt.int32

P = 128
B = 8
HID = 512
KT = HID // P
RANK = 16
SLOTS0, SLOTS1, SLOTS2 = 32, 16, 8
HQ, HK, D = 32, 8, 128
GROUP = HQ // HK
PAGES, PSIZE, NPP = 64, 32, 16
CACHE = NPP * PSIZE
CCH = CACHE // P
CH = CCH + 1
KEYS = CACHE + P
ROWS_PER_PAGE = PSIZE // CCH
UNITS = HK * B
WQKV = GROUP * D + 2 * D
WCOLS = KT * WQKV + GROUP * HID
WCH = WCOLS // B
AHEAD = B + 1
THETA = 10000.0
EPS = 1e-06
SCALE = 1.0 / float(np.sqrt(D))
LORA_SCALE = 2.0
NEG = -1e30
TWO_PI = 2.0 * np.pi
TURN_A = 6.28125
TURN_B = float(np.float32(np.round((TWO_PI - TURN_A) * 2.0**21) / 2.0**21))
TURN_C = float(TWO_PI - TURN_A - TURN_B)
ROUND_MAGIC = 1.5 * 2.0**23
PI_BELOW = float(np.nextafter(np.float32(np.pi), np.float32(0.0)))


def build(nc, x, x_t, ids0, ids1, ids2, table, lens, w0_t, bias0, lora_a, lora_b, w1_t, w2_b, w2_a,
          w_qkvo, q_norm, k_norm, k_rows, v_rows, inv_freq, row_in_table, ident_in, out):
    ctx = ExitStack()
    with ctx:
        def sem(name):
            return ctx.enter_context(nc.semaphore(name))

        def sb(name, shape, dt=F32, scope=ctx):
            return scope.enter_context(nc.sbuf_tensor(name, shape, dt))

        def pb(name, shape, scope=ctx):
            return scope.enter_context(nc.psum_tensor(name, shape, F32))

        w_hi = sb("w_hi", [P, 2, WCOLS], F32R)
        w_lo = sb("w_lo", [P, 2, WCOLS], F32R)
        w_raw = sb("w_raw", [P, 2, WCH])
        y = sb("y", [P, B, HID])
        cos_q = sb("cos_q", [P, B, D])
        sin_q = sb("sin_q", [P, B, D])
        cos_k = sb("cos_k", [P, B, D])
        sin_k = sb("sin_k", [P, B, D])
        ident = sb("ident", [P, P])
        pos = sb("pos", [P, CACHE])
        len_f = sb("len_f", [P, B])
        row_id = sb("row_id", [P, UNITS], I32)
        neg_half = sb("neg_half", [P, GROUP + 1])
        x_s = sb("x_s", [P, 2, HID], F32R)
        k_raw = sb("k_raw", [P, CCH * D])
        v_raw = sb("v_raw", [P, CCH * D])
        k_row = sb("k_row", [P, 1], I32)
        v_row = sb("v_row", [P, 1], I32)
        xt_dram = nc.dram_tensor("xt_split", [B, P, 2, HID], F32).ap()

        w_raw_in = sem("w_raw_in")
        w_split = sem("w_split")
        w_rounded = sem("w_rounded")
        x_s_in, k_in, v_in = sem("x_s_in"), sem("k_in"), sem("v_in")
        k_row_set, v_row_set, row_id_set = sem("k_row_set"), sem("v_row_set"), sem("row_id_set")
        tables_in = sem("tables_in")

        def w_home(chunk):
            return ((chunk >> 3) & 1) * WCOLS + (chunk & 7) * WCH

        w_hi_flat = w_hi[:, :, :].rearrange("p s c -> p (s c)")
        w_lo_flat = w_lo[:, :, :].rearrange("p s c -> p (s c)")

        def weight_high(copy, chunk, raw):
            return copy(w_hi_flat[:, bass.ds(w_home(chunk), WCH)], raw)

        def weight_low(chunk, raw):
            hi = w_hi_flat[:, bass.ds(w_home(chunk), WCH)]
            lo = w_lo_flat[:, bass.ds(w_home(chunk), WCH)]
            return nc.gpsimd.tensor_tensor(lo, raw, hi.bitcast(F32), ALU.subtract)


        with ExitStack() as p1:
            def slot(s):
                return s % 2

            def turns_of_slot(i, s):
                return i + s // 2 + 1

            w0_hi = sb("w0_hi", [P, KT, HID], F32R, scope=p1)
            w0_lo = sb("w0_lo", [P, KT, HID], F32R, scope=p1)
            w0_raw = y[:, B - KT:, :]
            w1 = sb("w1", [P, 2, KT, HID], scope=p1)
            xb = sb("xb", [P, 2, HID], scope=p1)
            xbt = sb("xbt", [P, 2, HID], scope=p1)
            xbt_hi = sb("xbt_hi", [P, HID], F32R, scope=p1)
            xbt_lo = sb("xbt_lo", [P, HID], F32R, scope=p1)
            a0 = sb("a0", [P, 2, KT, RANK], scope=p1)
            b0 = sb("b0", [RANK + 1, 2, HID], scope=p1)
            b2 = sb("b2", [P, 2, KT, RANK], scope=p1)
            a2 = sb("a2", [RANK, 2, HID], scope=p1)
            h0 = sb("h0", [RANK + 1, P], scope=p1)
            h2 = sb("h2", [RANK, P], scope=p1)
            x1 = sb("x1", [P, 2, HID], scope=p1)
            x2 = sb("x2", [P, 2, HID], scope=p1)
            x3 = sb("x3", [P, HID], scope=p1)
            x1t = sb("x1t", [P, HID], scope=p1)
            x2t = sb("x2t", [P, HID], scope=p1)
            x3t = sb("x3t", [P, 2, HID], F32R, scope=p1)
            ids = sb("ids", [1, 3, B], I32, scope=p1)
            exp_warm = sb("exp_warm", [P, 1], scope=p1)
            len_i = sb("len_i", [P, B], I32, scope=p1)
            tab_i = sb("tab_i", [P, B], I32, scope=p1)
            part_row = sb("part_row", [P, UNITS], I32, scope=p1)
            tab8 = sb("tab8", [P, B], I32, scope=p1)
            freq = sb("freq", [P, D // 2], scope=p1)
            wq_row = sb("wq_row", [P, D], scope=p1)
            wk_row = sb("wk_row", [P, D], scope=p1)
            wq_signed = sb("wq_signed", [P, D], scope=p1)
            wk_signed = sb("wk_signed", [P, D], scope=p1)
            row_f = sb("row_f", [P, B], scope=p1)
            sin_t = sb("sin_t", [P, B, D // 2], scope=p1)
            cos_t = sb("cos_t", [P, B, D // 2], scope=p1)
            ang = cos_k[:, :, 0:D // 2]
            whole_turns, taken = cos_k[:, :, D // 2:], cos_q[:, :, D // 2:]
            sin_arg, cos_arg = sin_k[:, :, 0:D // 2], cos_q[:, :, 0:D // 2]

            ps_h2 = pb("ps_h2", [P, HID], p1)
            ps_l2 = pb("ps_l2", [P, HID], p1)
            ps_t2 = pb("ps_t2", [P, HID], p1)
            ps_l1 = pb("ps_l1", [P, HID], p1)
            ps_t1 = pb("ps_t1", [P, HID], p1)
            ps_l0 = pb("ps_l0", [P, HID], p1)
            ps_h0 = pb("ps_h0", [P, HID], p1)
            ps_t3 = pb("ps_t3", [P, HID], p1)

            w0_in = [sem(f"w0_in_{k}") for k in range(KT)]
            ids_in, other_ids_in, bias_in, ident_in_place = (sem(s) for s in ("ids_in", "other_ids_in", "bias_in", "ident_in_place"))
            x_in, xt_in, ab0_in, w1_in, ab2_in = (
                [sem(f"{name}_{which}") for which in ("even", "odd")] for name in ("x_in", "xt_in", "ab0_in", "w1_in", "ab2_in"))
            ones_set = sem("ones_set")
            w0_hi_out, w0_lo_out = sem("w0_hi_out"), sem("w0_lo_out")
            xt_hi_out, xt_lo_out = sem("xt_hi_out"), sem("xt_lo_out")
            base_done, h0_done, h0_out, l0_done, x1_out = (sem(s) for s in ("base_done", "h0_done", "h0_out", "l0_done", "x1_out"))
            t1_done, t1_out, l1_done, x2_out = (sem(s) for s in ("t1_done", "t1_out", "l1_done", "x2_out"))
            t2_done, t2_out, h2_done, h2_out = (sem(s) for s in ("t2_done", "t2_out", "h2_done", "h2_out"))
            l2_done, x3_out, y_out, t3_done = (sem(s) for s in ("l2_done", "x3_out", "y_out", "t3_done"))
            t3_hi, t3_lo, xt_stored = (sem(s) for s in ("t3_hi", "t3_lo", "xt_stored"))
            tab8_set, pool_step, arg_set, trig_done, tables_set = (
                sem(s) for s in ("tab8_set", "pool_step", "arg_set", "trig_done", "tables_set"))
            w_first_in = [sem(f"w_first_in_{which}") for which in ("even", "odd")]

            def one(t, at):
                return t[bass.ds(at, 1)].rearrange("a p k r -> p (a k) r") if len(t.shape) == 4 else t[bass.ds(at, 1)].rearrange("a p c -> (a p) c")

        with ExitStack() as p2:
            rot_a = sb("rot_a", [P, GROUP + 1, D], scope=p2)
            rot_b = sb("rot_b", [P, GROUP + 1, D], scope=p2)
            rot = sb("rot", [P, GROUP + 1, D], scope=p2)
            key_sum = sb("key_sum", [P, D], scope=p2)
            junk = sb("junk", [P, GROUP + 1, D], scope=p2)
            sq = sb("sq", [P, GROUP + 1], scope=p2)
            var = sb("var", [P, GROUP + 1], scope=p2)
            rstd = sb("rstd", [P, GROUP + 1], scope=p2)
            q_gain = sb("q_gain", [P, GROUP], scope=p2)
            kt_hi = sb("kt_hi", [P, 2 * KEYS], F32R, scope=p2)
            kt_lo = sb("kt_lo", [P, 2 * KEYS], F32R, scope=p2)
            qt_hi = sb("qt_hi", [P, GROUP * P], F32R, scope=p2)
            qt_lo = sb("qt_lo", [P, GROUP * P], F32R, scope=p2)
            v_hi = sb("v_hi", [P, CH, D], F32R, scope=p2)
            v_lo = sb("v_lo", [P, CH, D], F32R, scope=p2)
            prob = sb("prob", [P, GROUP, KEYS], scope=p2)
            pt_hi = sb("pt_hi", [P, CH, GROUP * P], F32R, scope=p2)
            pt_lo = sb("pt_lo", [P, CH, GROUP * P], F32R, scope=p2)
            ot_hi = sb("ot_hi", [P, GROUP * P], F32R, scope=p2)
            ot_lo = sb("ot_lo", [P, GROUP * P], F32R, scope=p2)
            mask = sb("mask", [P, KEYS], scope=p2)
            low = sb("low", [P, GROUP], scope=p2)
            total = sb("total", [P, GROUP], scope=p2)
            inv = sb("inv", [P, GROUP], scope=p2)

            ps_s = pb("ps_s", [P, 3 * 512], p2)
            ps_ring = pb("ps_ring", [P, 2, 512], p2)
            ps_q = pb("ps_q", [P, 512], p2)
            ps_kv = pb("ps_kv", [P, 512], p2)
            ps_o = pb("ps_o", [P, 512], p2)

            mask_set = sem("mask_set")
            q_proj, kv_proj = sem("q_proj"), sem("kv_proj")
            sq_done, var_done, rstd_done, gain_done = (sem(s) for s in ("sq_done", "var_done", "rstd_done", "gain_done"))
            key_rotated = sem("key_rotated")
            q_rotated, q_summed, key_summed, key_scaled, rot_turned = (
                sem(s) for s in ("q_rotated", "q_summed", "key_summed", "key_scaled", "rot_turned"))
            qt_hi_out, qt_lo_out = sem("qt_hi_out"), sem("qt_lo_out")
            kc_turned, kc_hi_out, kc_lo_out = sem("kc_turned"), sem("kc_hi_out"), sem("kc_lo_out")
            v_hi_out, v_split, vn_hi_out, vn_lo_out = (sem(s) for s in ("v_round", "v_split", "vn_hi_out", "vn_lo_out"))
            scores, low_done, exp_done, inv_done, prob_done = (sem(s) for s in ("scores", "low_done", "exp_done", "inv_done", "prob_done"))
            p_turned, pt_hi_out, pt_lo_out = sem("p_turned"), sem("pt_hi_out"), sem("pt_lo_out")
            pv_done, ot_hi_out, ot_lo_out = sem("pv_done"), sem("ot_hi_out"), sem("ot_lo_out")
            out_proj, y_added, out_in = sem("out_proj"), sem("y_added"), sem("out_in")

            MIDDLE = KEYS - (512 - P)
            CUTS = ((KEYS - MIDDLE, KEYS), (0, KEYS - MIDDLE)), ((0, MIDDLE), (MIDDLE, KEYS))

            def keys_of(kt, u, lo, hi):
                return kt[:, bass.ds((u & 1) * KEYS + lo, hi - lo)]

            def score_slot(h):
                return P + (h % 2) * KEYS

            with nc.Block() as block:
                @block.sync
                def _(sp):
                    def first_input(i, s, first=False):
                        e, at = 2 * i + s, slot(s)
                        if not first:
                            sp.wait_ge(l0_done, e - 1)
                            sp.nop(nofuse=True)
                        if not first:
                            sp.dma_start(xbt[:, at, :], one(x_t, e)).then_inc(xt_in[at], 16)
                        id0 = sp.value_load(ids[0:1, 0, bass.ds(e, 1)], min_val=0, max_val=SLOTS0 - 1)
                        sp.dma_start(a0[:, at, :, :], one(lora_a, id0)).then_inc(ab0_in[at], 16)
                        sp.dma_start(b0[0:RANK, at, :], one(lora_b, id0)).then_inc(ab0_in[at], 16)
                        if not first:
                            sp.wait_ge(x1_out, e - 1)
                            sp.nop(nofuse=True)
                        sp.dma_start(xb[:, at, :], one(x, e)).then_inc(x_in[at], 16)

                    def second_weights(i, s, first=False):
                        e, at = 2 * i + s, slot(s)
                        if not first:
                            sp.wait_ge(l1_done, e - 1)
                            sp.nop(nofuse=True)
                        id1 = sp.value_load(ids[0:1, 1, bass.ds(e, 1)], min_val=0, max_val=SLOTS1 - 1)
                        sp.dma_start(w1[:, at, :, :], one(w1_t, id1)).then_inc(w1_in[at], 16)

                    def third_adapter(i, s, first=False):
                        e, at = 2 * i + s, slot(s)
                        if not first:
                            sp.wait_ge(l2_done, e - 1)
                            sp.nop(nofuse=True)
                        id2 = sp.value_load(ids[0:1, 2, bass.ds(e, 1)], min_val=0, max_val=SLOTS2 - 1)
                        sp.dma_start(b2[:, at, :, :], one(w2_b, id2)).then_inc(ab2_in[at], 16)
                        sp.dma_start(a2[:, at, :], one(w2_a, id2)).then_inc(ab2_in[at], 16)

                    sp.dma_start(xbt[:, 0, :], one(x_t, 0)).then_inc(xt_in[0], 16)
                    for k in range(KT):
                        sp.dma_start(w0_raw[:, k, :], w0_t[:, k, :]).then_inc(w0_in[k], 16)
                    sp.dma_start(xbt[:, 1, :], one(x_t, 1)).then_inc(xt_in[1], 16)
                    sp.wait_ge(ids_in, 16)
                    first_input(0, 0, first=True)
                    for at in (0, 1):
                        sp.dma_start(b0[RANK:RANK + 1, at, :], bias0).then_inc(bias_in, 16)
                    sp.dma_start(ids[:, 1, :], ids1).then_inc(other_ids_in, 16)
                    sp.dma_start(ids[:, 2, :], ids2).then_inc(other_ids_in, 16)
                    sp.dma_start(ident[:, :], ident_in).then_inc(ident_in_place, 16)
                    sp.wait_ge(other_ids_in, 32)
                    second_weights(0, 0, first=True)
                    first_input(0, 1, first=True)

                    def layers(i, s, input_next=True, weights_next=True, first=False, start=False):
                        if input_next:
                            first_input(i, s + 2)
                        if weights_next:
                            second_weights(i, s + 1, first=start)
                        third_adapter(i, s, first=first)

                    layers(0, 0, first=True, start=True)
                    layers(0, 1, first=True)
                    with sp.Fori(1, B // 2 - 1) as i:
                        layers(i, 0)
                        layers(i, 1)
                    layers(B // 2 - 1, 0, input_next=False)
                    layers(B // 2 - 1, 1, input_next=False, weights_next=False)
                    sp.wait_ge(xt_stored, 16)
                    sp.dma_start(x_s[:, :, :].bitcast(F32), xt_dram[0:1, :, :, :].rearrange("a p s c -> p (a s) c")).then_inc(x_s_in, 16)

                    def step(n, weights, last, finished):
                        if not last:
                            sp.wait_ge(kv_proj, n + 1)
                            sp.nop(nofuse=True)
                            sp.dma_start(x_s[:, :, :].bitcast(F32), xt_dram[bass.ds((n + 1) & 7, 1), :, :, :].rearrange("a p s c -> p (a s) c")).then_inc(x_s_in, 16)
                        if weights:
                            sp.wait_ge(w_split, n + AHEAD)
                            sp.dma_start(w_raw[:, 0, :], w_qkvo[bass.ds(n + AHEAD, 1), :, :].rearrange("a p c -> p (a c)")).then_inc(w_raw_in, 16)
                        if finished:
                            sp.wait_ge(y_added, n)
                            sp.nop(nofuse=True)
                            sp.dma_start(out[bass.ds((n - 1) & 7, 1), :, :].rearrange("a p c -> p (a c)"),
                                         y[:, bass.ds((n - 1) & 7, 1), :].rearrange("p a c -> p (a c)")).then_inc(out_in, 16)

                    sp.wait_ge(xt_stored, 32)
                    step(0, True, False, False)
                    sp.wait_ge(xt_stored, 16 * B)
                    with sp.Fori(1, UNITS - AHEAD) as n:
                        step(n, True, False, False)
                    with sp.Fori(UNITS - AHEAD, UNITS - B + 1) as n:
                        step(n, False, False, False)
                    with sp.Fori(UNITS - B + 1, UNITS - 1) as n:
                        step(n, False, False, True)
                    step(UNITS - 1, False, True, True)
                    step(UNITS, False, True, True)
                    sp.wait_ge(out_in, 16 * B)

                @block.gpsimd
                def _(pool):
                    steps = [0]

                    def step(ins):
                        steps[0] += 1
                        ins.then_inc(pool_step, 1)
                        pool.wait_ge(pool_step, steps[0])

                    nc.gpsimd.iota(pos[:, :], [[1, CCH], [CCH, P]], base=0, channel_multiplier=0,
                                   allow_small_or_imprecise_dtypes=True)
                    nc.gpsimd.memset(neg_half[:, :], -0.5)
                    pool.dma_start(len_i[:, :], lens.partition_broadcast(P)).then_inc(tables_in, 16)
                    pool.dma_start(freq[:, :], inv_freq.partition_broadcast(P)).then_inc(tables_in, 16)
                    pool.dma_start(tab_i[:, :], table).then_inc(tables_in, 16)
                    pool.dma_start(part_row[:, :], row_in_table).then_inc(tables_in, 16)
                    pool.dma_start(wq_row[:, :], q_norm.partition_broadcast(P)).then_inc(tables_in, 16)
                    pool.dma_start(wk_row[:, :], k_norm.partition_broadcast(P)).then_inc(tables_in, 16)

                    step(nc.gpsimd.iota(row_f[:, :], [[0, B]], base=0, channel_multiplier=1,
                                        allow_small_or_imprecise_dtypes=True))
                    pool.wait_ge(tables_in, 16 * 6)
                    step(nc.gpsimd.tensor_copy(len_f[:, :], len_i[:, :]))
                    step(nc.gpsimd.tensor_tensor(row_f[:, :], row_f[:, :], len_f[:, :], ALU.add))
                    step(nc.gpsimd.tensor_tensor(
                        ang, row_f[:, :].rearrange("p (b d) -> p b d", d=1).broadcast_to([P, B, D // 2]),
                        freq[:, :].rearrange("p (b d) -> p b d", b=1).broadcast_to([P, B, D // 2]), ALU.mult))
                    for quarter, arg in ((0, sin_arg), (1, cos_arg)):
                        step(nc.gpsimd.tensor_scalar(whole_turns, ang, 1.0 / TWO_PI, 0.25 * quarter, ALU.mult, ALU.add))
                        step(nc.gpsimd.tensor_scalar(whole_turns, whole_turns, ROUND_MAGIC, ROUND_MAGIC, ALU.add, ALU.subtract))
                        left = ang
                        for part in (TURN_A, TURN_B, TURN_C):
                            step(nc.gpsimd.tensor_scalar(taken, whole_turns, part, None, ALU.mult))
                            step(nc.gpsimd.tensor_tensor(arg, left, taken, ALU.subtract))
                            left = arg
                        step(nc.gpsimd.tensor_scalar(arg, arg, 0.5 * np.pi * quarter, PI_BELOW, ALU.add, ALU.min))
                        step(nc.gpsimd.tensor_scalar(arg, arg, -PI_BELOW, None, ALU.max))
                    nc.gpsimd.tensor_copy(wq_signed[:, 0:D // 2], wq_row[:, 0:D // 2])
                    nc.gpsimd.tensor_scalar(wq_signed[:, D // 2:], wq_row[:, D // 2:], -1.0, None, ALU.mult)
                    nc.gpsimd.tensor_copy(wk_signed[:, 0:D // 2], wk_row[:, 0:D // 2])
                    nc.gpsimd.tensor_scalar(wk_signed[:, D // 2:], wk_row[:, D // 2:], -1.0, None, ALU.mult).then_inc(arg_set, 1)

                    pool.wait_ge(row_id_set, 1)
                    for row, row_set, raw, rows, arrived in ((k_row, k_row_set, k_raw, k_rows, k_in), (v_row, v_row_set, v_raw, v_rows, v_in)):
                        nc.gpsimd.tensor_copy(row[:, :], row_id[:, 0:1]).then_inc(row_set, 1)
                        pool.wait_ge(row_set, 1)
                        nc.gpsimd.indirect_dma_start(
                            raw[:, :], None, rows, bass.IndirectOffsetOnAxis(row[:, 0:1], axis=0)).then_inc(arrived, 16)

                    def load_chunk(j, at):
                        pool.dma_start(w_raw[:, at, :], one(w_qkvo, 2 * j + at)).then_inc(w_first_in[at], 16)

                    def split_chunk(j, at):
                        c = 2 * j + at
                        pool.wait_ge(w_first_in[at], 16 * (j + 1))
                        pool.nop(nofuse=True)
                        weight_high(nc.gpsimd.tensor_copy, c, w_raw[:, at, :]).then_inc(w_rounded, 1)
                        pool.wait_ge(w_rounded, c + 1)
                        weight_low(c, w_raw[:, at, :]).then_inc(w_split, 1)

                    load_chunk(0, 0)
                    load_chunk(0, 1)
                    with pool.Fori(0, (AHEAD - 1) // 2 - 1) as j:
                        for at in (0, 1):
                            split_chunk(j, at)
                            pool.wait_ge(w_split, 2 * j + at + 1)
                            pool.nop(nofuse=True)
                            load_chunk(j + 1, at)
                    split_chunk(AHEAD // 2 - 1, 0)
                    pool.wait_ge(w_split, AHEAD - 2)
                    load_chunk(AHEAD // 2, 0)
                    split_chunk(AHEAD // 2 - 1, 1)
                    split_chunk(AHEAD // 2, 0)

                    def gather(u, row, row_set, raw, rows, arrived):
                        pool.wait_ge(arrived, 16 * u)
                        pool.nop(nofuse=True)
                        nc.gpsimd.tensor_copy(row[:, :], row_id[:, bass.ds(u, 1)]).then_inc(row_set, 1)
                        pool.wait_ge(row_set, u + 1)
                        pool.nop(nofuse=True)
                        nc.gpsimd.indirect_dma_start(
                            raw[:, :], None, rows, bass.IndirectOffsetOnAxis(row[:, 0:1], axis=0)).then_inc(arrived, 16)

                    def next_keys(u):
                        pool.wait_ge(kc_turned, u)
                        gather(u, k_row, k_row_set, k_raw, k_rows, k_in)

                    def next_values(u):
                        pool.wait_ge(v_split, u)
                        gather(u, v_row, v_row_set, v_raw, v_rows, v_in)

                    def sum_queries(u, first=False):
                        pool.wait_ge(q_rotated, u + 1)
                        if not first:
                            pool.wait_ge(rot_turned, u)
                        nc.gpsimd.tensor_tensor(rot[:, 0:GROUP, :], rot_a[:, 0:GROUP, :], rot_b[:, 0:GROUP, :], ALU.add).then_inc(q_summed, 1)

                    def norm_factors(u):
                        pool.wait_ge(var_done, u + 1)
                        nc.gpsimd.tensor_tensor(rstd[:, :], var[:, :], neg_half[:, :], ALU.pow).then_inc(rstd_done, 1)

                    def step(n, weights, keys, last):
                        vl = v_lo[:, 0:CCH, :].rearrange("p c d -> p (c d)")
                        vh = v_hi[:, 0:CCH, :].rearrange("p c d -> p (c d)")
                        pool.wait_ge(v_hi_out, n + 1)
                        nc.gpsimd.tensor_tensor(vl, v_raw[:, :], vh.bitcast(F32), ALU.subtract).then_inc(v_split, 1)
                        if not last:
                            next_values(n + 1)
                        if keys:
                            next_keys(n + 2)
                        if not last:
                            sum_queries(n + 1)
                            norm_factors(n + 1)
                        if weights:
                            pool.wait_ge(w_rounded, n + AHEAD + 1)
                            weight_low(n + AHEAD, w_raw[:, 0, :]).then_inc(w_split, 1)

                    sum_queries(0, first=True)
                    norm_factors(0)
                    next_keys(1)
                    with pool.Fori(0, UNITS - AHEAD) as n:
                        step(n, True, True, False)
                    with pool.Fori(UNITS - AHEAD, UNITS - 2) as n:
                        step(n, False, True, False)
                    step(UNITS - 2, False, False, False)
                    step(UNITS - 1, False, False, True)

                @block.scalar
                def _(act):
                    def copy(dst, src):
                        return nc.scalar.activation(dst, src, ACT.Copy)

                    act.dma_start(ids[:, 0, :], ids0).then_inc(ids_in, 16)

                    def input_high(i, s, first=False):
                        act.wait_ge(xt_in[slot(s)], 16 * turns_of_slot(i, s))
                        if not first:
                            act.wait_ge(base_done, 2 * i + s)
                        copy(xbt_hi[:, :], xbt[:, slot(s), :]).then_inc(xt_hi_out, 1)

                    def lora_high(e, first=False):
                        act.wait_ge(h0_done, e + 1)
                        if not first:
                            act.wait_ge(l0_done, e)
                        nc.scalar.activation(h0[0:RANK, :], ps_h0[0:RANK, 0:P], ACT.Copy, scale=LORA_SCALE).then_inc(h0_out, 1)

                    def first_turned(e, first=False):
                        act.wait_ge(t1_done, e + 1)
                        if not first:
                            act.wait_ge(l1_done, e)
                        copy(x1t[:, :], ps_t1[:, :]).then_inc(t1_out, 1)

                    def second_turned(e, first=False):
                        act.wait_ge(t2_done, e + 1)
                        if not first:
                            act.wait_ge(h2_done, e)
                        copy(x2t[:, :], ps_t2[:, :]).then_inc(t2_out, 1)

                    def second_low_rank(e, first=False):
                        act.wait_ge(h2_done, e + 1)
                        if not first:
                            act.wait_ge(l2_done, e)
                        copy(h2[:, :], ps_h2[0:RANK, 0:P]).then_inc(h2_out, 1)

                    def third_turned(e, first=False):
                        act.wait_ge(t3_done, e + 1)
                        if not first:
                            act.wait_ge(xt_stored, 16 * e)
                        copy(x3t[:, 0, :], ps_t3[:, :]).then_inc(t3_hi, 1)

                    def store(e):
                        act.wait_ge(t3_lo, e + 1)
                        act.dma_start(one(xt_dram, e), x3t[:, :, :].bitcast(F32)).then_inc(xt_stored, 16)

                    def layers(i, s, t2=True, t1=True, stored=True, h0_next=True, input_next=True, first=False, second=False):
                        t = 2 * i + s
                        if t2:
                            second_turned(t - 1, first=second)
                        if t1:
                            first_turned(t, first=first)
                        if stored:
                            store(t - 2)
                        if t2:
                            second_low_rank(t - 1, first=second)
                        if h0_next:
                            lora_high(t + 1)
                        if input_next:
                            input_high(i, s + 2)
                        if t2:
                            third_turned(t - 1, first=second)

                    input_high(0, 0, first=True)
                    for k in range(KT):
                        act.wait_ge(w0_in[k], 16)
                        copy(w0_hi[:, k, :], w0_raw[:, k, :]).then_inc(w0_hi_out, 1)
                    lora_high(0, first=True)
                    input_high(0, 1)
                    layers(0, 0, t2=False, stored=False, first=True)
                    layers(0, 1, stored=False, second=True)
                    with act.Fori(1, B // 2 - 1) as i:
                        layers(i, 0)
                        layers(i, 1)
                    act.wait_ge(arg_set, 1)
                    nc.scalar.activation(sin_t[:, :, :], sin_arg, ACT.Sin)
                    nc.scalar.activation(cos_t[:, :, :], cos_arg, ACT.Sin).then_inc(trig_done, 1)
                    layers(B // 2 - 1, 0, input_next=False)
                    layers(B // 2 - 1, 1, h0_next=False, input_next=False)
                    nc.scalar.activation(exp_warm[:, :], ident[:, 0:1], ACT.Exp)

                    def copy(dst, src):
                        return nc.scalar.activation(dst, src, ACT.Copy)

                    def square(src, h):
                        nc.scalar.activation(junk[:, h, :], src, ACT.Square, accum_out=sq[:, h:h + 1]).then_inc(sq_done, 1)

                    def query_squares(u, heads, first=False):
                        act.wait_ge(q_rotated, u + 1)
                        if not first:
                            act.wait_ge(var_done, u)
                        for h in heads:
                            square(ps_q[:, h * D:(h + 1) * D], h)

                    def key_squares(u):
                        act.wait_ge(kv_proj, u + 1)
                        square(ps_kv[:, 0:D], GROUP)

                    def scale_key(u):
                        act.wait_ge(key_summed, u + 1)
                        act.wait_ge(rstd_done, u + 1)
                        nc.scalar.activation(rot[:, GROUP, :], key_sum[:, :], ACT.Copy, scale=rstd[:, GROUP:GROUP + 1]).then_inc(key_scaled, 1)

                    def cached_high(u, first=False):
                        act.wait_ge(kc_turned, u + 1)
                        if not first:
                            act.wait_ge(scores, GROUP * (u - 1))
                        copy(keys_of(kt_hi, u, 0, CACHE), ps_ring[:, 0, :]).then_inc(kc_hi_out, 1)

                    def rotated_high(u):
                        act.wait_ge(rot_turned, u + 1)
                        copy(qt_hi[:, :], ps_q[:, :])
                        copy(keys_of(kt_hi, u, CACHE, KEYS), ps_kv[:, 2 * D:3 * D]).then_inc(qt_hi_out, 1)

                    def out_high(u):
                        act.wait_ge(pv_done, u + 1)
                        copy(ot_hi[:, :], ps_o[:, :]).then_inc(ot_hi_out, 1)

                    def exps(n, h):
                        act.wait_ge(low_done, GROUP * n + h + 1)
                        nc.scalar.activation(prob[:, h, :], prob[:, h, :], ACT.Exp, bias=low[:, h:h + 1], scale=-1.0,
                                             accum_out=total[:, h:h + 1]).then_inc(exp_done, 1)

                    def normalize(n, h):
                        act.wait_ge(inv_done, GROUP * n + h + 1)
                        nc.scalar.activation(prob[:, h, :], prob[:, h, :], ACT.Copy, scale=inv[:, h:h + 1]).then_inc(prob_done, 1)

                    def chunk_high(n, c, bank):
                        act.wait_ge(p_turned, CH * n + c + 1)
                        copy(pt_hi[:, c, :], ps_ring[:, bank, :]).then_inc(pt_hi_out, 1)

                    def step(n, keys, last, first=False):
                        if first:
                            cached_high(1, first=True)
                        else:
                            out_high(n - 1)
                        act.wait_ge(qt_lo_out, n + 1)
                        copy(v_hi[:, CCH, :], ps_kv[:, D:2 * D]).then_inc(vn_hi_out, 1)
                        exps(n, 0)
                        exps(n, 1)
                        normalize(n, 0)
                        normalize(n, 1)
                        exps(n, 2)
                        exps(n, 3)
                        normalize(n, 2)
                        normalize(n, 3)
                        if not last:
                            query_squares(n + 1, (0, 1))
                        chunk_high(n, 0, 1)
                        chunk_high(n, 1, 0)
                        if not last:
                            query_squares(n + 1, (2, 3))
                            key_squares(n + 1)
                        chunk_high(n, 2, 1)
                        if not last:
                            scale_key(n + 1)
                        chunk_high(n, 3, 0)
                        chunk_high(n, 4, 1)
                        if not last:
                            rotated_high(n + 1)
                        if keys:
                            cached_high(n + 2)

                    store(B - 2)
                    second_turned(B - 1)
                    query_squares(0, range(GROUP), first=True)
                    key_squares(0)
                    second_low_rank(B - 1)
                    cached_high(0, first=True)
                    scale_key(0)
                    rotated_high(0)
                    third_turned(B - 1)
                    store(B - 1)
                    step(0, True, False, first=True)
                    with act.Fori(1, UNITS - 2) as n:
                        step(n, True, False)
                    step(UNITS - 2, False, False)
                    step(UNITS - 1, False, True)
                    out_high(UNITS - 1)

                @block.tensor
                def _(pe):
                    def turn(dst, src, done):
                        for k in range(KT):
                            mm = nc.tensor.transpose(dst[:, k * P:(k + 1) * P], src[:, k * P:(k + 1) * P], ident[:, :])
                        mm.then_inc(done, 1)

                    def three(dst, lhs, rhs, first, final):
                        (lh, ll), (rh, rl) = lhs, rhs
                        nc.tensor.matmul(dst, lh, rh, start=first, stop=False)
                        nc.tensor.matmul(dst, lh, rl, start=False, stop=False)
                        return nc.tensor.matmul(dst, ll, rh, start=False, stop=final)

                    def base(e, first=False):
                        pe.wait_ge(xt_lo_out, e + 1)
                        for k in range(KT):
                            if first:
                                pe.wait_ge(w0_lo_out, k + 1)
                            cut = slice(k * P, (k + 1) * P)
                            mm = three(ps_l0[:, :], (xbt_hi[:, cut], xbt_lo[:, cut]), (w0_hi[:, k, :], w0_lo[:, k, :]), k == 0, False)
                        mm.then_inc(base_done, 1)

                    def lora_in(i, s):
                        at = slot(s)
                        pe.wait_ge(ab0_in[at], 32 * turns_of_slot(i, s))
                        for k in range(KT):
                            mm = nc.tensor.matmul(ps_h0[0:RANK, 0:P], a0[:, at, k, :], xbt[:, at, k * P:(k + 1) * P],
                                                  start=(k == 0), stop=(k == KT - 1))
                        mm.then_inc(h0_done, 1)

                    def lora_out(e, at):
                        pe.wait_ge(h0_out, e + 1)
                        nc.tensor.matmul(ps_l0[:, :], h0[:, :], b0[:, at, :], start=False, stop=True).then_inc(l0_done, 1)

                    def layer_1(i, s):
                        at = slot(s)
                        pe.wait_ge(w1_in[at], 16 * turns_of_slot(i, s))
                        pe.wait_ge(t1_out, 2 * i + s + 1)
                        for k in range(KT):
                            mm = nc.tensor.matmul(ps_l1[:, :], x1t[:, k * P:(k + 1) * P], w1[:, at, k, :],
                                                  start=(k == 0), stop=(k == KT - 1))
                        mm.then_inc(l1_done, 1)

                    def layer_2_in(i, s):
                        at = slot(s)
                        pe.wait_ge(t2_out, 2 * i + s + 1)
                        pe.wait_ge(ab2_in[at], 32 * turns_of_slot(i, s))
                        for k in range(KT):
                            mm = nc.tensor.matmul(ps_h2[0:RANK, 0:P], b2[:, at, k, :], x2t[:, k * P:(k + 1) * P],
                                                  start=(k == 0), stop=(k == KT - 1))
                        mm.then_inc(h2_done, 1)

                    def layer_2_out(e, at):
                        pe.wait_ge(h2_out, e + 1)
                        nc.tensor.matmul(ps_l2[:, :], h2[:, :], a2[:, at, :], start=True, stop=True).then_inc(l2_done, 1)

                    def layers(i, s, l0=True, l1=True, l2=True, second=False):
                        t = 2 * i + s
                        if l2:
                            pe.wait_ge(x2_out, t)
                            turn(ps_t2, x2[:, slot(s - 1), :], t2_done)
                        if l1:
                            pe.wait_ge(x1_out, t + 1)
                            turn(ps_t1, x1[:, slot(s), :], t1_done)
                        if l0:
                            base(t + 1)
                        if l2:
                            layer_2_in(i, s - 1)
                        if l0:
                            lora_in(i, s + 1)
                        if l1:
                            layer_1(i, s)
                        if l2:
                            layer_2_out(t - 1, slot(s - 1))
                        if l0:
                            lora_out(t + 1, slot(s + 1))
                        if l2:
                            pe.wait_ge(x3_out, t)
                            if not second:
                                pe.wait_ge(t3_lo, t - 1)
                            turn(ps_t3, x3, t3_done)

                    base(0, first=True)
                    lora_in(0, 0)
                    pe.wait_ge(ones_set, 1)
                    pe.wait_ge(bias_in, 32)
                    lora_out(0, 0)
                    pe.wait_ge(ident_in_place, 16)
                    layers(0, 0, l2=False)
                    layers(0, 1, second=True)
                    with pe.Fori(1, B // 2 - 1) as i:
                        layers(i, 0)
                        layers(i, 1)
                    layers(B // 2 - 1, 0)
                    layers(B // 2 - 1, 1, l0=False)

                    def weight_rows(unit, at, size):
                        home = ((unit >> 3) & 1) * WCOLS + at
                        return w_hi_flat[:, bass.ds(home, size)], w_lo_flat[:, bass.ds(home, size)]

                    def project(dst, u, at, size, products=range(3 * KT)):
                        for i in products:
                            k = i // 3
                            w, w_rest = weight_rows(u, k * WQKV + at, size)
                            mm = nc.tensor.matmul(dst, x_s[:, int(i % 3 == 2), k * P:(k + 1) * P], w_rest if i % 3 == 1 else w,
                                                  start=i == 0, stop=i == 3 * KT - 1)
                        return mm

                    QUERY_CUT = 8

                    def project_queries(u, first=False):
                        pe.wait_ge(x_s_in, 16 * (u + 1))
                        if not first:
                            pe.wait_ge(w_split, ((u >> 3) << 3) + B)
                            pe.wait_ge(qt_lo_out, u)
                        project(ps_q[:, :], u, 0, GROUP * D, range(QUERY_CUT))

                    def project_queries_rest(u):
                        project(ps_q[:, :], u, 0, GROUP * D, range(QUERY_CUT, 3 * KT)).then_inc(q_proj, 1)

                    def project_new_key(u, first=False):
                        if not first:
                            pe.wait_ge(vn_lo_out, u)
                        project(ps_kv[:, 0:2 * D], u, GROUP * D, 2 * D).then_inc(kv_proj, 1)

                    def turn_cached(u):
                        pe.wait_ge(k_in, 16 * (u + 1))
                        for c in range(CCH):
                            mm = nc.tensor.transpose(ps_ring[:, 0, c * P:(c + 1) * P], k_raw[:, c * D:(c + 1) * D], ident[:, :])
                        mm.then_inc(kc_turned, 1)

                    def turn_rotated(u):
                        pe.wait_ge(q_summed, u + 1)
                        pe.wait_ge(key_scaled, u + 1)
                        for h in range(GROUP):
                            nc.tensor.transpose(ps_q[:, h * P:(h + 1) * P], rot[:, h, :], ident[:, :])
                        nc.tensor.transpose(ps_kv[:, 2 * D:3 * D], rot[:, GROUP, :], ident[:, :]).then_inc(rot_turned, 1)

                    def score_pair(n, pair):
                        pe.wait_ge(low_done, GROUP * n + 2 * pair)
                        heads = 2 * pair, 2 * pair + 1

                        def part(h, piece):
                            lo, hi = CUTS[h % 2][piece]
                            q = qt_hi[:, h * P:(h + 1) * P], qt_lo[:, h * P:(h + 1) * P]
                            return three(ps_s[:, score_slot(h) + lo:score_slot(h) + hi], q,
                                         (keys_of(kt_hi, n, lo, hi), keys_of(kt_lo, n, lo, hi)), True, True)

                        for h in heads:
                            part(h, 0)
                        for h in heads:
                            part(h, 1).then_inc(scores, 1)

                    def put_out(u):
                        pe.wait_ge(ot_lo_out, u + 1)
                        for h in range(GROUP):
                            ot = ot_hi[:, h * P:(h + 1) * P], ot_lo[:, h * P:(h + 1) * P]
                            mm = three(ps_o[:, :], ot, weight_rows(u, KT * WQKV + h * HID, HID), h == 0, h == GROUP - 1)
                        mm.then_inc(out_proj, 1)

                    def turn_probs(n, c, bank, heads=range(GROUP)):
                        for h in heads:
                            mm = nc.tensor.transpose(ps_ring[:, bank, h * P:(h + 1) * P], prob[:, h, c * P:(c + 1) * P], ident[:, :])
                        if h == GROUP - 1:
                            mm.then_inc(p_turned, 1)

                    def values(n, c):
                        pe.wait_ge(pt_lo_out, CH * n + c + 1)
                        mm = three(ps_o[:, :], (v_hi[:, c, :], v_lo[:, c, :]), (pt_hi[:, c, :], pt_lo[:, c, :]),
                                   c == 0, c == CH - 1)
                        if c == CH - 1:
                            mm.then_inc(pv_done, 1)

                    def step(n, keys, last, first=False):
                        if first:
                            pe.wait_ge(kc_lo_out, 1)
                            turn_cached(1)
                        pe.wait_ge(qt_lo_out, n + 1)
                        pe.wait_ge(kc_lo_out, n + 1)
                        score_pair(n, 0)
                        if not last:
                            project_queries(n + 1)
                        score_pair(n, 1)
                        if not last:
                            project_queries_rest(n + 1)
                        if not first:
                            put_out(n - 1)
                        early, late = range(GROUP - 1), (GROUP - 1,)
                        pe.wait_ge(prob_done, GROUP * n + GROUP - 1)
                        turn_probs(n, 0, 1, early)
                        pe.wait_ge(kc_lo_out, n + 1 if last else n + 2)
                        turn_probs(n, 1, 0, early)
                        pe.wait_ge(prob_done, GROUP * n + GROUP)
                        turn_probs(n, 0, 1, late)
                        turn_probs(n, 1, 0, late)
                        if not last:
                            project_new_key(n + 1)
                        pe.wait_ge(v_split, n + 1)
                        pe.wait_ge(vn_lo_out, n + 1)
                        if not first:
                            pe.wait_ge(y_added, n)
                        pe.wait_ge(pt_lo_out, CH * n + 1)
                        turn_probs(n, 2, 1)
                        values(n, 0)
                        pe.wait_ge(pt_lo_out, CH * n + 2)
                        turn_probs(n, 3, 0)
                        values(n, 1)
                        pe.wait_ge(pt_lo_out, CH * n + 3)
                        turn_probs(n, 4, 1)
                        if not last:
                            turn_rotated(n + 1)
                        values(n, 2)
                        if keys:
                            pe.wait_ge(pt_lo_out, CH * n + 4)
                            turn_cached(n + 2)
                        values(n, 3)
                        values(n, 4)

                    pe.wait_ge(w_split, B)
                    project_queries(0, first=True)
                    project_queries_rest(0)
                    project_new_key(0, first=True)
                    pe.wait_ge(x2_out, B)
                    turn(ps_t2, x2[:, slot(B - 1), :], t2_done)
                    turn_cached(0)
                    layer_2_in(B // 2 - 1, 1)
                    layer_2_out(B - 1, slot(B - 1))
                    turn_rotated(0)
                    pe.wait_ge(x3_out, B)
                    pe.wait_ge(t3_lo, B - 1)
                    turn(ps_t3, x3, t3_done)
                    step(0, True, False, first=True)
                    with pe.Fori(1, UNITS - 2) as n:
                        step(n, True, False)
                    step(UNITS - 2, False, False)
                    step(UNITS - 1, False, True)
                    put_out(UNITS - 1)

                @block.vector
                def _(dve):
                    def rest(dst, src, high):
                        return nc.vector.tensor_tensor(dst, src, high.bitcast(F32), ALU.subtract)

                    def input_low(i, s):
                        dve.wait_ge(xt_hi_out, 2 * i + s + 1)
                        rest(xbt_lo[:, :], xbt[:, slot(s), :], xbt_hi[:, :]).then_inc(xt_lo_out, 1)

                    def third_turned(e):
                        dve.wait_ge(t3_hi, e + 1)
                        rest(x3t[:, 1, :], ps_t3[:, :], x3t[:, 0, :]).then_inc(t3_lo, 1)

                    def first_sum(i, s):
                        dve.wait_ge(l0_done, 2 * i + s + 1)
                        dve.wait_ge(x_in[slot(s)], 16 * turns_of_slot(i, s))
                        nc.vector.tensor_tensor(x1[:, slot(s), :], ps_l0[:, :], xb[:, slot(s), :], ALU.add).then_inc(x1_out, 1)

                    def second_sum(e, at):
                        dve.wait_ge(l1_done, e + 1)
                        nc.vector.tensor_tensor(x2[:, at, :], ps_l1[:, :], x1[:, at, :], ALU.add).then_inc(x2_out, 1)

                    def third_sum(e, at, first=False):
                        dve.wait_ge(l2_done, e + 1)
                        if not first:
                            dve.wait_ge(y_out, e)
                        nc.vector.tensor_tensor(x3[:, :], ps_l2[:, :], x2[:, at, :], ALU.add).then_inc(x3_out, 1)

                    def keep_sum(e):
                        dve.wait_ge(x3_out, e + 1)
                        nc.vector.tensor_copy(y[:, bass.ds(e, 1), :].rearrange("p a c -> p (a c)"), x3[:, :]).then_inc(y_out, 1)

                    def rotary_tables(w, signed, cs, sn):
                        half = D // 2

                        def wide(w, cut):
                            return w[:, cut].rearrange("p (b d) -> p b d", b=1).broadcast_to([P, B, half])

                        for here, there in ((slice(0, half), slice(half, D)), (slice(half, D), slice(0, half))):
                            nc.vector.tensor_tensor(cs[:, :, here], cos_t[:, :, :], wide(w, here), ALU.mult)
                            ins = nc.vector.tensor_tensor(sn[:, :, here], sin_t[:, :, :], wide(signed, there), ALU.mult)
                        ins.then_inc(tables_set, 1)

                    def layers(i, s, l0=True, l1=True, l2=True, input_next=True, second=False):
                        t = 2 * i + s
                        if input_next:
                            input_low(i, s + 2)
                        if l1:
                            second_sum(t, slot(s))
                        if l2:
                            dve.wait_ge(x2_out, t)
                            third_sum(t - 1, slot(s - 1), first=second)
                        if l0:
                            dve.wait_ge(x2_out, t)
                            first_sum(i, s + 1)
                        if l2:
                            keep_sum(t - 1)
                        if l2:
                            third_turned(t - 1)

                    nc.vector.memset(h0[:, :], 1.0).then_inc(ones_set, 1)
                    input_low(0, 0)
                    for k in range(KT):
                        dve.wait_ge(w0_hi_out, k + 1)
                        rest(w0_lo[:, k, :], w0_raw[:, k, :], w0_hi[:, k, :]).then_inc(w0_lo_out, 1)
                    first_sum(0, 0)
                    input_low(0, 1)
                    dve.wait_ge(tables_in, 16 * 6)
                    nc.vector.tensor_scalar(tab8[:, :], tab_i[:, :], float(ROWS_PER_PAGE), None, ALU.mult).then_inc(tab8_set, 1)
                    dve.wait_ge(tab8_set, 1)
                    nc.vector.tensor_tensor(
                        row_id[:, :].rearrange("p (g b) -> p g b", g=HK), part_row[:, :].rearrange("p (g b) -> p g b", g=HK),
                        tab8[:, :].rearrange("p (g b) -> p g b", g=1).broadcast_to([P, HK, B]), ALU.add).then_inc(row_id_set, 1)
                    layers(0, 0, l2=False)
                    layers(0, 1, second=True)
                    with dve.Fori(1, B // 2 - 1) as i:
                        layers(i, 0)
                        layers(i, 1)
                    layers(B // 2 - 1, 0, input_next=False)
                    dve.wait_ge(trig_done, 1)
                    rotary_tables(wq_row, wq_signed, cos_q, sin_q)
                    layers(B // 2 - 1, 1, l0=False, input_next=False)

                    def rest(dst, src, high):
                        return nc.vector.tensor_tensor(dst, src, high.bitcast(F32), ALU.subtract)

                    def set_mask(u):
                        nc.vector.tensor_scalar(mask[:, 0:CACHE], pos[:, :], len_f[:, bass.ds(u & 7, 1)], NEG,
                                                ALU.is_ge, ALU.mult).then_inc(mask_set, 1)

                    def halves(u, table, heads):
                        for o in (0, D // 2):
                            yield slice(o, o + D // 2), slice(D // 2 - o, D - o), table[:, bass.ds(u & 7, 1), o:o + D // 2].broadcast_to([P, heads, D // 2])

                    def rotate_queries(u, first=False):
                        dve.wait_ge(q_proj, u + 1)
                        if not first:
                            dve.wait_ge(q_summed, u)
                        q = ps_q[:, :].rearrange("p (h d) -> p h d", h=GROUP)
                        nc.vector.tensor_tensor(rot_a[:, 0:GROUP, :], q, cos_q[:, bass.ds(u & 7, 1), :].broadcast_to([P, GROUP, D]), ALU.mult)

                    def rotate_queries_rest(u):
                        q = ps_q[:, :].rearrange("p (h d) -> p h d", h=GROUP)
                        for here, there, sines in halves(u, sin_q, GROUP):
                            ins = nc.vector.tensor_tensor(rot_b[:, 0:GROUP, here], q[:, :, there], sines, ALU.mult)
                        ins.then_inc(q_rotated, 1)

                    def variances(u, first=False):
                        dve.wait_ge(sq_done, (GROUP + 1) * (u + 1))
                        if not first:
                            dve.wait_ge(rstd_done, u)
                        nc.vector.tensor_scalar(var[:, :], sq[:, :], 1.0 / D, EPS, ALU.mult, ALU.add).then_inc(var_done, 1)

                    def rotate_key(u, first=False):
                        if not first:
                            dve.wait_ge(key_scaled, u)
                        key = ps_kv[:, 0:D].rearrange("p (h d) -> p h d", h=1)
                        nc.vector.tensor_tensor(rot_a[:, GROUP:, :], key, cos_k[:, bass.ds(u & 7, 1), :], ALU.mult)
                        for here, there, sines in halves(u, sin_k, 1):
                            ins = nc.vector.tensor_tensor(rot_b[:, GROUP:, here], key[:, :, there], sines, ALU.mult)
                        ins.then_inc(key_rotated, 1)
                        dve.wait_ge(key_rotated, u + 1)
                        nc.vector.tensor_tensor(key_sum[:, :], rot_a[:, GROUP, :], rot_b[:, GROUP, :], ALU.add).then_inc(key_summed, 1)

                    def gains(u):
                        dve.wait_ge(rstd_done, u + 1)
                        nc.vector.tensor_scalar(q_gain[:, :], rstd[:, 0:GROUP], -SCALE, None, ALU.mult).then_inc(gain_done, 1)

                    def values_high(n, first=False):
                        dve.wait_ge(v_in, 16 * (n + 1))
                        if not first:
                            dve.wait_ge(pv_done, n)
                        nc.vector.tensor_copy(v_hi[:, 0:CCH, :].rearrange("p c d -> p (c d)"), v_raw[:, :]).then_inc(v_hi_out, 1)

                    def weights_high(n):
                        dve.wait_ge(w_raw_in, 16 * (n + 1))
                        weight_high(nc.vector.tensor_copy, n + AHEAD, w_raw[:, 0, :]).then_inc(w_rounded, 1)

                    def cached_low(u):
                        dve.wait_ge(kc_hi_out, u + 1)
                        rest(keys_of(kt_lo, u, 0, CACHE), ps_ring[:, 0, :], keys_of(kt_hi, u, 0, CACHE)).then_inc(kc_lo_out, 1)

                    def rotated_low(u):
                        dve.wait_ge(qt_hi_out, u + 1)
                        rest(qt_lo[:, :], ps_q[:, :], qt_hi[:, :])
                        rest(keys_of(kt_lo, u, CACHE, KEYS), ps_kv[:, 2 * D:3 * D], keys_of(kt_hi, u, CACHE, KEYS)).then_inc(qt_lo_out, 1)

                    def out_low(u):
                        dve.wait_ge(ot_hi_out, u + 1)
                        rest(ot_lo[:, :], ps_o[:, :], ot_hi[:, :]).then_inc(ot_lo_out, 1)

                    def lowest(n, h):
                        dve.wait_ge(scores, GROUP * n + h + 1)
                        dve.nop(nofuse=True)
                        nc.vector.tensor_tensor_reduce(
                            out=prob[:, h, :], in0=ps_s[:, score_slot(h):score_slot(h) + KEYS], in1=mask[:, :], scale=q_gain[:, h:h + 1], scalar=3.0e38,
                            op0=ALU.add, op1=ALU.min, accum_out=low[:, h:h + 1]).then_inc(low_done, 1)

                    def inverse(n, h):
                        dve.wait_ge(exp_done, GROUP * n + h + 1)
                        nc.vector.reciprocal(inv[:, h:h + 1], total[:, h:h + 1]).then_inc(inv_done, 1)

                    def add_out(u):
                        dve.wait_ge(out_proj, u + 1)
                        yb = y[:, bass.ds(u & 7, 1), :].rearrange("p a c -> p (a c)")
                        nc.vector.tensor_tensor(yb, ps_o[:, :], yb, ALU.add).then_inc(y_added, 1)

                    def chunk_low(n, c, bank):
                        dve.wait_ge(pt_hi_out, CH * n + c + 1)
                        rest(pt_lo[:, c, :], ps_ring[:, bank, :], pt_hi[:, c, :]).then_inc(pt_lo_out, 1)

                    def step(n, weights, last, first=False):
                        if not first:
                            out_low(n - 1)
                        dve.wait_ge(mask_set, n + 1)
                        dve.wait_ge(gain_done, n + 1)
                        if not first:
                            dve.wait_ge(p_turned, CH * n)
                        lowest(n, 0)
                        lowest(n, 1)
                        inverse(n, 0)
                        values_high(n, first)
                        inverse(n, 1)
                        dve.wait_ge(vn_hi_out, n + 1)
                        rest(v_lo[:, CCH, :], ps_kv[:, D:2 * D], v_hi[:, CCH, :]).then_inc(vn_lo_out, 1)
                        lowest(n, 2)
                        lowest(n, 3)
                        if not last:
                            cached_low(n + 1)
                        inverse(n, 2)
                        if not last:
                            rotate_queries(n + 1)
                        inverse(n, 3)
                        if not last:
                            rotate_queries_rest(n + 1)
                        if not first:
                            add_out(n - 1)
                        if weights:
                            weights_high(n)
                        chunk_low(n, 0, 1)
                        chunk_low(n, 1, 0)
                        if not last:
                            variances(n + 1)
                            rotate_key(n + 1)
                        chunk_low(n, 2, 1)
                        chunk_low(n, 3, 0)
                        chunk_low(n, 4, 1)
                        if not last:
                            rotated_low(n + 1)
                            gains(n + 1)
                            dve.wait_ge(low_done, GROUP * (n + 1))
                            set_mask(n + 1)

                    dve.wait_ge(tables_set, 1)
                    rotate_queries(0, first=True)
                    rotate_queries_rest(0)
                    rotary_tables(wk_row, wk_signed, cos_k, sin_k)
                    variances(0, first=True)
                    dve.wait_ge(tables_set, 2)
                    rotate_key(0, first=True)
                    dve.wait_ge(x2_out, B)
                    third_sum(B - 1, slot(B - 1))
                    gains(0)
                    cached_low(0)
                    rotated_low(0)
                    keep_sum(B - 1)
                    third_turned(B - 1)
                    dve.wait_ge(y_out, B)
                    nc.vector.memset(mask[:, CACHE:], 0.0)
                    set_mask(0)
                    step(0, True, False, first=True)
                    with dve.Fori(1, UNITS - AHEAD) as n:
                        step(n, True, False)
                    with dve.Fori(UNITS - AHEAD, UNITS - 1) as n:
                        step(n, False, False)
                    step(UNITS - 1, False, True)
                    out_low(UNITS - 1)
                    add_out(UNITS - 1)


def kernel(x, itok_B_0_23, itok_B_0_15, itok_B_3_7, itok_Bx16_0_63, itok_B_207_1644, L0_cond_W, L0_cond_b,
           L0_cond_lora_As, L0_cond_lora_Bs, L1_cond_weight, L2_cond_A, L2_cond_B, L3_cond_Wq, L3_cond_Wk,
           L3_cond_Wv, L3_cond_Wo, L3_cond_q_norm_w, L3_cond_k_norm_w, L3_cond_k_cache, L3_cond_v_cache):
    import concourse.bacc as bacc
    from concourse.bass_utils import run_bass_kernel_spmd

    def tiles(a):
        a = np.asarray(a)
        a = a.reshape(*a.shape[:-2], KT, P, a.shape[-1])
        return np.moveaxis(a, -3, -2)

    def swap(a):
        return np.swapaxes(np.asarray(a), -1, -2)

    wq = tiles(swap(L3_cond_Wq)).reshape(P, KT, HK, GROUP * D)
    wk = tiles(swap(L3_cond_Wk)).reshape(P, KT, HK, D)
    wv = tiles(swap(L3_cond_Wv)).reshape(P, KT, HK, D)
    qkv = np.concatenate([wq, wk, wv], axis=3).transpose(2, 0, 1, 3).reshape(HK, P, KT * WQKV)
    wo = swap(L3_cond_Wo).reshape(HK, GROUP, D, HID).transpose(0, 2, 1, 3).reshape(HK, P, GROUP * HID)
    w_qkvo = np.concatenate([qkv, wo], axis=2).reshape(HK, P, B, WCH).transpose(0, 2, 1, 3).reshape(UNITS, P, WCH)

    def cache_rows(a):
        a = np.asarray(a).reshape(PAGES, ROWS_PER_PAGE, CCH, HK, D)
        return a.transpose(3, 0, 1, 2, 4).reshape(HK * PAGES * ROWS_PER_PAGE, CCH * D)

    part = np.arange(P)[:, None]
    unit = np.arange(UNITS)[None, :]
    f32 = np.float32
    inv_freq = (f32(1.0) / f32(THETA) ** (np.arange(0, D, 2, dtype=f32) / f32(D))).astype(f32)
    arrays = {
        "x": np.asarray(x),
        "x_t": tiles(swap(x)).reshape(B, P, HID),
        "ids0": np.asarray(itok_B_0_23).reshape(1, B),
        "ids1": np.asarray(itok_B_0_15).reshape(1, B),
        "ids2": np.asarray(itok_B_3_7).reshape(1, B),
        "table": np.repeat(np.asarray(itok_Bx16_0_63).T, ROWS_PER_PAGE, axis=0),
        "lens": np.asarray(itok_B_207_1644),
        "w0_t": tiles(swap(L0_cond_W)),
        "bias0": np.asarray(L0_cond_b).reshape(1, HID),
        "lora_a": tiles(L0_cond_lora_As),
        "lora_b": np.asarray(L0_cond_lora_Bs),
        "w1_t": tiles(swap(L1_cond_weight)),
        "w2_b": tiles(swap(L2_cond_B)),
        "w2_a": swap(L2_cond_A),
        "w_qkvo": w_qkvo,
        "q_norm": np.asarray(L3_cond_q_norm_w),
        "k_norm": np.asarray(L3_cond_k_norm_w),
        "k_rows": cache_rows(L3_cond_k_cache),
        "v_rows": cache_rows(L3_cond_v_cache),
        "inv_freq": inv_freq,
        "row_in_table": (part % ROWS_PER_PAGE + (unit // B) * PAGES * ROWS_PER_PAGE).astype(np.int32),
        "ident_in": np.eye(P, dtype=f32),
    }
    nc = bacc.Bacc("TRN2", target_bir_lowering=False, num_devices=1)
    sent, args = {}, []
    for name, a in arrays.items():
        a = np.ascontiguousarray(a)
        sent[f"{name}_dram"] = a
        args.append(nc.dram_tensor(f"{name}_dram", a.shape, mybir.dt.from_np(a.dtype), kind="ExternalInput").ap())
    args.append(nc.dram_tensor("out_dram", (B, P, HID), F32, kind="ExternalOutput").ap())
    build(nc, *args)
    r = run_bass_kernel_spmd(nc, [sent], core_ids=[0])
    return r.results[0]["out_dram"]
```
